# Optimizing a Trainium2 kernel written in Bass

```python
import numpy as np
import jax
import jax.numpy as jnp

def _softmax(x, axis=-1):
    return jax.nn.softmax(x, axis=axis)

def _gelu(x):
    return jax.nn.gelu(x, approximate=True)

def _silu(x):
    return jax.nn.silu(x)

def _sigmoid(x):
    return jax.nn.sigmoid(x)

def _layernorm(x, axis=-1, eps=1e-05):
    m = jnp.mean(x, axis=axis, keepdims=True)
    v = jnp.var(x, axis=axis, keepdims=True)
    return (x - m) / jnp.sqrt(v + eps)

def _scatter_add(tgt, idx, src, axis=0):
    return tgt.at[idx].add(src)

def _segment_sum(src, seg, n):
    return jax.ops.segment_sum(src, seg, n)
kernel_name = 'mk_decoder_postln_d1_seqx_r8_868f24'

def setup_inputs(seed: int=0):
    np.random.seed(seed)
    _w = jnp.asarray

    def _rec_inputs():
        import jax
        import jax.numpy as jnp
        _rk = jax.random.key(seed)
        x = -0.0002928 + 1 * jax.random.normal(jax.random.fold_in(_rk, 1), (128, 64, 128), jnp.float32)
        _lenS = 64 - jax.random.randint(jax.random.fold_in(_rk, 7), (128,), 0, max(1, 64 // 4) + 1, jnp.int32)
        _lenS2 = 64 - jax.random.randint(jax.random.fold_in(_rk, 8), (128,), 0, max(1, 64 // 4) + 1, jnp.int32)
        _ctx_1024P = jax.random.normal(jax.random.fold_in(_rk, 11), (128, 16, 128), jnp.float32)
        _ctx_1024c = jax.random.dirichlet(jax.random.fold_in(_rk, 511), 0.3 * jnp.ones((16,), jnp.float32), (128, 64))
        _ctx_1024t = jnp.einsum('bsk,bkd->bsd', _ctx_1024c, _ctx_1024P)
        _ctx_1024t = _ctx_1024t * jax.lax.rsqrt(jnp.mean(jnp.square(_ctx_1024t)) + 1e-12) * 0.953939
        ctx_1024 = -1.39393e-06 + 0.999914 * (_ctx_1024t + 0.3 * jax.random.normal(jax.random.fold_in(_rk, 611), (128, 64, 128), jnp.float32))
        return (x, ctx_1024)
    x, ctx_1024 = _rec_inputs()

    def _L0_attn_setup():
        import jax, jax.numpy as jnp
        import numpy as np
        D_MODEL = 128
        NUM_HEADS = 16
        BATCH = 2
        SEQ = 256

        def _trunc_normal(key, shape, std):
            return jax.random.truncated_normal(key, -3.0, 3.0, shape, dtype=jnp.float32) * std
        key = jax.random.key(seed)
        kx, kq, kk, kv, ko = jax.random.split(key, 5)
        std = (2.0 / (D_MODEL + D_MODEL)) ** 0.5
        return {'X': jax.random.normal(kx, (BATCH, SEQ, D_MODEL), dtype=jnp.float32), 'q_proj': _trunc_normal(kq, (D_MODEL, D_MODEL), std), 'k_proj': _trunc_normal(kk, (D_MODEL, D_MODEL), std), 'v_proj': _trunc_normal(kv, (D_MODEL, D_MODEL), std), 'o_proj': _trunc_normal(ko, (D_MODEL, D_MODEL), std)}
    _L0_attn_all = _L0_attn_setup()
    _L0_attn_in = {k: v for k, v in _L0_attn_all.items() if k in ('q_proj', 'k_proj', 'v_proj', 'o_proj')}
    del _L0_attn_all

    def _L0_xattn_setup():
        import jax, jax.numpy as jnp
        import numpy as np
        SCALE_BASE = 512.0
        GN_EPS = 1e-05

        def _xpos(x, downscale):
            L, D = (x.shape[-2], x.shape[-1])
            half = D // 2
            base = (jnp.arange(0, D, 2, dtype=jnp.float32) + 0.4 * D) / (1.4 * D)
            min_pos = -(L // 2)
            power = (jnp.arange(min_pos, min_pos + L, dtype=jnp.float32) / SCALE_BASE)[:, None]
            scale = base[None, :] ** power
            inv_freq = 1.0 / 10000.0 ** (jnp.arange(half, dtype=jnp.float32) / half)
            ang = jnp.arange(L, dtype=jnp.float32)[:, None] * inv_freq[None, :]
            sin, cos = (jnp.sin(ang), jnp.cos(ang))
            if downscale:
                scale = 1.0 / scale
            sin_s = jnp.repeat(sin * scale, 2, axis=-1)
            cos_s = jnp.repeat(cos * scale, 2, axis=-1)
            x1, x2 = (x[..., ::2], x[..., 1::2])
            rot = jnp.stack((-x2, x1), axis=-1).reshape(x.shape)
            return x * cos_s + rot * sin_s

        def _decay_mask(L, H):
            gammas = 1.0 - jnp.exp(jnp.linspace(np.log(1.0 / 32.0), np.log(1.0 / 512.0), H)).astype(jnp.float32)
            idx = jnp.arange(L)
            dist = idx[:, None] - idx[None, :]
            causal = dist >= 0
            d = jnp.maximum(dist, 0).astype(jnp.float32)
            return jnp.where(causal[None], gammas[:, None, None] ** d[None], 0.0)
        key = jax.random.key(seed)
        ks = jax.random.split(key, 9)
        B, L, D, H = (2, 256, 128, 16)
        hd = D // H
        return {'query': jax.random.normal(ks[0], (B, L, D), jnp.float32), 'key': jax.random.normal(ks[1], (B, L, D), jnp.float32), 'value': jax.random.normal(ks[2], (B, L, D), jnp.float32), 'W_Q': jax.random.normal(ks[3], (H, D, hd), jnp.float32) / D, 'W_K': jax.random.normal(ks[4], (H, D, hd), jnp.float32) / D, 'W_V': jax.random.normal(ks[5], (H, D, hd), jnp.float32) / D, 'g_w': jax.random.normal(ks[6], (D, D), jnp.float32) * (2.0 / (D + D)) ** 0.5, 'g_b': jnp.zeros((D,), jnp.float32), 'out_w': jax.random.normal(ks[7], (D, D), jnp.float32) * (2.0 / (D + D)) ** 0.5, 'out_b': jnp.zeros((D,), jnp.float32)}
    _L0_xattn_all = _L0_xattn_setup()
    _L0_xattn_in = {k: v for k, v in _L0_xattn_all.items() if k in ('W_Q', 'W_K', 'W_V', 'g_w', 'g_b', 'out_w', 'out_b')}
    del _L0_xattn_all

    def _L0_ffn_setup():
        import jax, jax.numpy as jnp
        import numpy as np
        DMODEL = 128
        N_EXPERTS = 32
        EXPERT_SIZE = 64
        N_HEADS = 4
        WEIGHT_SCALE = 1.0
        key = jax.random.key(seed)
        k0, k1, k2, k3 = jax.random.split(key, 4)
        x = jax.random.normal(k0, (2, 256, DMODEL), dtype=jnp.float32)
        expert_sel = jax.random.normal(k1, (N_EXPERTS, DMODEL), dtype=jnp.float32) * DMODEL ** (-0.5)
        keys = jax.random.normal(k2, (N_EXPERTS, DMODEL, EXPERT_SIZE), dtype=jnp.float32) * DMODEL ** (-0.5)
        values = jax.random.normal(k3, (N_EXPERTS, EXPERT_SIZE, DMODEL), dtype=jnp.float32) * (N_EXPERTS * EXPERT_SIZE) ** (-0.5)
        return {'x': x, 'expert_sel': expert_sel, 'keys': keys, 'values': values}
    _L0_ffn_all = _L0_ffn_setup()
    _L0_ffn_in = {k: v for k, v in _L0_ffn_all.items() if k in ('expert_sel', 'keys', 'values')}
    del _L0_ffn_all
    return {'x': x, 'ctx_1024': ctx_1024, 'L0_attn_q_proj': _L0_attn_in['q_proj'], 'L0_attn_k_proj': _L0_attn_in['k_proj'], 'L0_attn_v_proj': _L0_attn_in['v_proj'], 'L0_attn_o_proj': _L0_attn_in['o_proj'], 'L0_xattn_W_Q': _L0_xattn_in['W_Q'], 'L0_xattn_W_K': _L0_xattn_in['W_K'], 'L0_xattn_W_V': _L0_xattn_in['W_V'], 'L0_xattn_g_w': _L0_xattn_in['g_w'], 'L0_xattn_g_b': _L0_xattn_in['g_b'], 'L0_xattn_out_w': _L0_xattn_in['out_w'], 'L0_xattn_out_b': _L0_xattn_in['out_b'], 'L0_ffn_expert_sel': _L0_ffn_in['expert_sel'], 'L0_ffn_keys': _L0_ffn_in['keys'], 'L0_ffn_values': _L0_ffn_in['values']}

def reference(x, ctx_1024, L0_attn_q_proj, L0_attn_k_proj, L0_attn_v_proj, L0_attn_o_proj, L0_xattn_W_Q, L0_xattn_W_K, L0_xattn_W_V, L0_xattn_g_w, L0_xattn_g_b, L0_xattn_out_w, L0_xattn_out_b, L0_ffn_expert_sel, L0_ffn_keys, L0_ffn_values):
    import jax
    import jax.numpy as jnp

    def _L0_attn_ref(X, q_proj, k_proj, v_proj, o_proj):
        import jax, jax.numpy as jnp
        import numpy as np
        D_MODEL = 128
        NUM_HEADS = 16
        BATCH = 2
        SEQ = 256

        def _trunc_normal(key, shape, std):
            return jax.random.truncated_normal(key, -3.0, 3.0, shape, dtype=jnp.float32) * std
        B, S, D = X.shape
        H = NUM_HEADS
        d_k = D // H
        q_w = q_proj.reshape(H, d_k, D)
        k_w = k_proj.reshape(H, d_k, D)
        v_w = v_proj.reshape(H, d_k, D)
        o_w = o_proj.reshape(D, H, d_k).transpose(1, 0, 2)
        q = jnp.einsum('hkd,bsd->bhsk', q_w, X)
        k = jnp.einsum('hkd,bsd->bhsk', k_w, X)
        v = jnp.einsum('hkd,bsd->bhsk', v_w, X)
        scale = 1.0 / jnp.sqrt(jnp.asarray(d_k, dtype=X.dtype))
        scores = jnp.einsum('bhqk,bhsk->bhqs', q, k) * scale
        causal = jnp.tril(jnp.ones((S, S), dtype=bool))
        scores = jnp.where(causal, scores, jnp.asarray(-jnp.inf, dtype=scores.dtype))
        attn = jax.nn.softmax(scores, axis=-1)
        attn_out = jnp.einsum('bhqs,bhsk->bhqk', attn, v)
        return jnp.einsum('hdv,bhsv->bsd', o_w, attn_out)

    def _L0_xattn_ref(query, key, value, W_Q, W_K, W_V, g_w, g_b, out_w, out_b):
        import jax, jax.numpy as jnp
        import numpy as np
        SCALE_BASE = 512.0
        GN_EPS = 1e-05

        def _xpos(x, downscale):
            L, D = (x.shape[-2], x.shape[-1])
            half = D // 2
            base = (jnp.arange(0, D, 2, dtype=jnp.float32) + 0.4 * D) / (1.4 * D)
            min_pos = -(L // 2)
            power = (jnp.arange(min_pos, min_pos + L, dtype=jnp.float32) / SCALE_BASE)[:, None]
            scale = base[None, :] ** power
            inv_freq = 1.0 / 10000.0 ** (jnp.arange(half, dtype=jnp.float32) / half)
            ang = jnp.arange(L, dtype=jnp.float32)[:, None] * inv_freq[None, :]
            sin, cos = (jnp.sin(ang), jnp.cos(ang))
            if downscale:
                scale = 1.0 / scale
            sin_s = jnp.repeat(sin * scale, 2, axis=-1)
            cos_s = jnp.repeat(cos * scale, 2, axis=-1)
            x1, x2 = (x[..., ::2], x[..., 1::2])
            rot = jnp.stack((-x2, x1), axis=-1).reshape(x.shape)
            return x * cos_s + rot * sin_s

        def _decay_mask(L, H):
            gammas = 1.0 - jnp.exp(jnp.linspace(np.log(1.0 / 32.0), np.log(1.0 / 512.0), H)).astype(jnp.float32)
            idx = jnp.arange(L)
            dist = idx[:, None] - idx[None, :]
            causal = dist >= 0
            d = jnp.maximum(dist, 0).astype(jnp.float32)
            return jnp.where(causal[None], gammas[:, None, None] ** d[None], 0.0)
        B, L, D = query.shape
        H = W_Q.shape[0]
        q = jnp.einsum('bld,hde->bhle', query, W_Q)
        k = jnp.einsum('bld,hde->bhle', key, W_K)
        v = jnp.einsum('bld,hde->bhle', value, W_V)
        q = _xpos(q, downscale=False)
        k = _xpos(k, downscale=True)
        sim = jnp.einsum('bhnd,bhsd->bhns', q, k) * _decay_mask(L, H)[None]
        ret = jnp.einsum('bhns,bhsd->bhnd', sim, v)
        mu = ret.mean(axis=-1, keepdims=True)
        var = ret.var(axis=-1, keepdims=True)
        ret = (ret - mu) / jnp.sqrt(var + GN_EPS)
        ret = ret.transpose(0, 2, 1, 3).reshape(B, L, D)
        gate = jax.nn.silu(query @ g_w.T + g_b)
        return ret * gate @ out_w.T + out_b

    def _L0_ffn_ref(x, expert_sel, keys, values):
        import jax, jax.numpy as jnp
        import numpy as np
        DMODEL = 128
        N_EXPERTS = 32
        EXPERT_SIZE = 64
        N_HEADS = 4
        WEIGHT_SCALE = 1.0
        B, S, D = x.shape
        xt = x.reshape(-1, D)
        N = xt.shape[0]
        sel_logits = jnp.einsum('nd,ed->ne', xt, expert_sel)
        gates = jax.nn.sigmoid(sel_logits)
        sel_val, sel_idx = jax.lax.top_k(gates, N_HEADS)
        gate_full = jnp.zeros_like(gates).at[jnp.arange(N)[:, None], sel_idx].set(sel_val)
        scores = jax.nn.relu(jnp.einsum('nd,edf->nef', xt, keys))
        scores = scores * gate_full[:, :, None]
        out = jnp.einsum('nef,efv->nv', scores, values)
        return out.reshape(B, S, -1)
    x = _layernorm(x + _L0_attn_ref(x, L0_attn_q_proj, L0_attn_k_proj, L0_attn_v_proj, L0_attn_o_proj), axis=-1)
    x = _layernorm(x + _L0_xattn_ref(x, ctx_1024, ctx_1024, L0_xattn_W_Q, L0_xattn_W_K, L0_xattn_W_V, L0_xattn_g_w, L0_xattn_g_b, L0_xattn_out_w, L0_xattn_out_b), axis=-1)
    x = _layernorm(x + _L0_ffn_ref(x, L0_ffn_expert_sel, L0_ffn_keys, L0_ffn_values), axis=-1)
    return x

_drawn_inputs = setup_inputs


def setup_inputs(seed=0):
    import zlib

    import numpy as np

    out = dict(_drawn_inputs(seed))
    spreads = {'L0_xattn_g_b': (0.0, 0.1), 'L0_xattn_out_b': (0.0, 0.1)}
    factors = {}
    for name, (base, spread) in spreads.items():
        noise = np.random.default_rng([zlib.crc32(name.encode()), seed]).standard_normal(out[name].shape)
        drawn = base * np.exp(spread * noise) if base else spread * noise
        out[name] = jnp.asarray(drawn.astype(out[name].dtype))
    for name, factor in factors.items():
        out[name] = (out[name] * factor).astype(out[name].dtype)
    return out
```

```python
import concourse.bass as bass
from concourse import mybir
from contextlib import ExitStack


def decoder_layer(nc: bass.Bass, x, ctx_in, q_proj, k_proj, v_proj, o_proj, W_Q, W_K, W_V, g_w, g_b,
                  out_w, out_b, expert_sel, keys, values, consts, out):
    f32 = mybir.dt.float32
    ALU = mybir.AluOpType
    ACT = mybir.ActivationFunctionType
    AX = mybir.AxisListType

    BATCH, S, D = x.shape
    H, _, HD = W_Q.shape
    E, _, F = keys.shape
    P = 128
    TOK = 512
    TILES = BATCH * S // TOK
    PAIRS = TOK // P
    SEQS = TOK // S
    QUADS = 4
    UNITS = 2
    BLOCKS = E * F // P
    TOP = 4
    MAX8 = 8
    SCALE = float(HD) ** -0.5

    x_tiles = x.rearrange("b s d -> (b s) d").rearrange("(t c p) d -> t p c d", c=PAIRS, p=P)
    ctx_tiles = ctx_in.rearrange("b s d -> (b s) d").rearrange("(t c p) d -> t p c d", c=PAIRS, p=P)
    out_tiles = out.rearrange("b s d -> (b s) d").rearrange("(t c p) d -> t p c d", c=PAIRS, p=P)
    gate_rows = nc.dram_tensor("gate_rows", (E, TOK), f32, kind="Internal").ap()

    stack = ExitStack()
    with stack:
        def sb(name, shape):
            return stack.enter_context(nc.sbuf_tensor(name, shape, f32))

        def ps(name):
            return stack.enter_context(nc.psum_tensor(name, [P, 512], f32))

        def sem(name):
            return stack.enter_context(nc.semaphore(name))

        const = sb("const", [P, consts.shape[1]])
        col = [0]

        def part(n):
            col[0] += n
            return const[:, col[0] - n:col[0]]

        ident = part(P)
        centre = part(P)
        head_mean = part(P)
        causal = part(S)
        decay = part(8 * S)
        q_cos, q_sin, k_cos, k_sin = part(S), part(S), part(S), part(S)
        head_pick = part(4)
        eps = part(1)

        raw_w = sb("raw_w", [P, 7, P])
        wT = sb("wT", [P, 7, P])
        wqT, wkT, wvT, woT, wgT, wouT, selT = (wT[:, n, :] for n in range(7))
        wq2, wk2, wv2 = sb("wq2", [P, P]), sb("wk2", [P, P]), sb("wv2", [P, P])
        wq2r, wk2r = sb("wq2r", [P, P]), sb("wk2r", [P, P])
        keys_sb = sb("keys_sb", [P, E, F])
        vals_sb = sb("vals_sb", [P, BLOCKS, P])
        gb, gb_neg = sb("gb", [P, 1]), sb("gb_neg", [P, 1])
        ob = sb("ob", [P, P])

        x_tok, c_tok = sb("x_tok", [P, PAIRS, D]), sb("c_tok", [P, PAIRS, D])
        xT, cT = sb("xT", [P, TOK]), sb("cT", [P, TOK])
        qT, kT = sb("qT", [P, TOK]), sb("kT", [P, TOK])
        k_exp = sb("k_exp", [P, 4, TOK])
        v_pad = [sb(f"v_pad{a}", [P, 2, 16, 4, 16]) for a in range(2)]
        probs = [sb(f"probs{r}", [P, 512]) for r in range(QUADS)]
        probsT = [sb(f"probsT{r}", [P, 512]) for r in range(QUADS)]
        row_max = sb("row_max", [P, QUADS, 8])
        row_sum = sb("row_sum", [P, PAIRS, QUADS, 4])
        row_inv = sb("row_inv", [P, PAIRS, H])
        inv_wide = sb("inv_wide", [P, PAIRS, H, HD])
        invT, attnT = sb("invT", [P, TOK]), sb("attnT", [P, TOK])
        h_tok = sb("h_tok", [P, PAIRS, D])
        x1_tok, x1b_tok, x1T = sb("x1_tok", [P, PAIRS, D]), sb("x1b_tok", [P, PAIRS, D]), sb("x1T", [P, TOK])
        stats, moments = sb("stats", [P, PAIRS, 6]), sb("moments", [P, PAIRS, 2])
        var_ln, rstd = sb("var_ln", [P, PAIRS]), sb("rstd", [P, PAIRS])
        stats3, moments3 = sb("stats3", [P, PAIRS, 6]), sb("moments3", [P, PAIRS, 2])
        var_ln3, rstd3 = sb("var_ln3", [P, PAIRS]), sb("rstd3", [P, PAIRS])
        k2c, k2s, q2c, q2s = sb("k2c", [P, TOK]), sb("k2s", [P, TOK]), sb("q2c", [P, TOK]), sb("q2s", [P, TOK])
        k2T, q2T = sb("k2T", [P, TOK]), sb("q2T", [P, TOK])
        k2_exp = sb("k2_exp", [P, SEQS, 4, S])
        simT = [sb(f"simT{r}", [P, 512]) for r in range(QUADS)]
        sw_rec = sb("sw_rec", [P, TOK])
        swish, swish_d, gateT = sb("swish", [P, TOK]), sb("swish_d", [P, TOK]), sb("gateT", [P, TOK])
        retT, cenT, sqT = sb("retT", [P, TOK]), sb("cenT", [P, TOK]), sb("sqT", [P, TOK])
        gvar, grs, ggate, gated = sb("gvar", [P, TOK]), sb("grs", [P, TOK]), sb("ggate", [P, TOK]), sb("gated", [P, TOK])
        x2_tok, x2T = sb("x2_tok", [P, PAIRS, D]), sb("x2T", [P, TOK])
        sel_e, sel_d = sb("sel_e", [P, PAIRS, E]), sb("sel_d", [P, PAIRS, E])
        sel_g = sb("sel_g", [P, PAIRS, E + MAX8 - TOP])
        sel_m = sb("sel_m", [P, PAIRS, E + MAX8 - TOP])
        tops = sb("tops", [P, PAIRS, MAX8])
        gates, gatesT = sb("gates", [P, PAIRS, E]), sb("gatesT", [P, P])
        gate_bc = sb("gate_bc", [P, BLOCKS, TOK])
        hidden = [sb(f"hidden{n}", [P, TOK]) for n in range(2)]
        yT = sb("yT", [P, TOK])
        h3_tok, out_tok = sb("h3_tok", [P, PAIRS, D]), sb("out_tok", [P, PAIRS, D])

        spare = sb("spare", [P, 1])
        W = [ps(f"work{r}") for r in range(QUADS)]
        O = ps("attn_out")
        HB = [ps("hid0"), ps("hid1")]
        Y = ps("expert_sum")

        consts_in, raw_in, w2_in, experts_in, bias_in = (sem(n) for n in (
            "consts_in", "raw_in", "w2_in", "experts_in", "bias_in"))
        x_in, c_in = sem("x_in"), sem("c_in")
        zeros_set, raw_zero, pads_set = sem("zeros_set"), sem("raw_zero"), sem("pads_set")
        w_turned, w_copied, w_rot = sem("w_turned"), sem("w_copied"), sem("w_rot")
        pe_xT, pe_cT, pe_k, pe_q = sem("pe_xT"), sem("pe_cT"), sem("pe_k"), sem("pe_q")
        xT_set, cT_set, kT_set, qT_set = sem("xT_set"), sem("cT_set"), sem("kT_set"), sem("qT_set")
        k_exp_set = sem("k_exp_set")
        pe_v, v_set = sem("pe_v"), sem("v_set")
        pe_scores = sem("pe_scores")
        masked, max_set, shifted, exp_set, sum_set = (sem(n) for n in (
            "masked", "max_set", "shifted", "exp_set", "sum_set"))
        pe_probsT, probsT_set = sem("pe_probsT"), sem("probsT_set")
        pe_attn = sem("pe_attn")
        inv_set, wide_set, pe_inv, invT_set, attnT_set = (sem(n) for n in (
            "inv_set", "wide_set", "pe_inv", "invT_set", "attnT_set"))
        pe_o, h1_set = sem("pe_o"), sem("h1_set")
        st_set, mo_set, ln_set, rs_set = sem("st_set"), sem("mo_set"), sem("ln_set"), sem("rs_set")
        x1_set, x1b_set, pe_x1T, x1T_set = sem("x1_set"), sem("x1b_set"), sem("pe_x1T"), sem("x1T_set")
        pe_k2, k2_mul, k2_set, k2_exp_set = sem("pe_k2"), sem("k2_mul"), sem("k2_set"), sem("k2_exp_set")
        pe_v2, v2_set = sem("pe_v2"), sem("v2_set")
        pe_q2, q2_mul, q2_set = sem("pe_q2"), sem("q2_mul"), sem("q2_set")
        pe_gate, sw_exp, sw_add, sw_inv, gate_set = (sem(n) for n in (
            "pe_gate", "sw_exp", "sw_add", "sw_inv", "gate_set"))
        pe_sim, decayed = sem("pe_sim"), sem("decayed")
        pe_ret, retT_set = sem("pe_ret"), sem("retT_set")
        pe_cen, cen_set, sq_set, pe_var, gvar_set, grs_set, ggate_set, gated_set = (sem(n) for n in (
            "pe_cen", "cen_set", "sq_set", "pe_var", "gvar_set", "grs_set", "ggate_set", "gated_set"))
        pe_out, h2_set, x2_set, pe_x2T, x2T_set = (sem(n) for n in (
            "pe_out", "h2_set", "x2_set", "pe_x2T", "x2T_set"))
        pe_sel, sel_exp, sel_add, sel_inv, top_set, top_cut, matched, gates_set = (sem(n) for n in (
            "pe_sel", "sel_exp", "sel_add", "sel_inv", "top_set", "top_cut", "matched", "gates_set"))
        pe_gates, gatesT_set = sem("pe_gates"), sem("gatesT_set")
        gates_out, gates_in = sem("gates_out"), sem("gates_in")
        pe_hid, hid_set, pe_y, yT_set = sem("pe_hid"), sem("hid_set"), sem("pe_y"), sem("yT_set")
        pe_ytok, h3_set = sem("pe_ytok"), sem("h3_set")
        st3_set, mo3_set, ln3_set, rs3_set, out_set = (sem(n) for n in (
            "st3_set", "mo3_set", "ln3_set", "rs3_set", "out_set"))
        stored = sem("stored")

        block = stack.enter_context(nc.Block())

        def over_tiles(engine, tile):
            tile(0, True, False)
            with engine.Fori(1, TILES) as i:
                tile(i, True, True)
            tile(TILES, False, True)

        FILL = {"start": 2, "after_v": 1, "scores0": 3, "scores1": 2, "norm": 2, "x1": 2,
                "sim": 1, "group": 1, "var": 1, "out": 1}
        assert sum(FILL.values()) == BLOCKS
        first_block = {}
        for key, n in FILL.items():
            first_block[key] = sum(list(FILL.values())[:list(FILL).index(key)])

        def blocks_at(key):
            return range(first_block[key], first_block[key] + FILL[key])

        def wait_apart(engine, fixed, count, semaphore, value):
            engine.wait_ge(fixed, count)
            engine.wait_ge(semaphore, value)

        @block.sync
        def _(sp):
            sp.sem_inc(stored, 16)
            sp.dma_start(const[:, :], consts).then_inc(consts_in, 16)
            sp.dma_start(x_tok[:, :, :], x_tiles[0]).then_inc(x_in, 16)
            sp.dma_start(c_tok[:, :, :], ctx_tiles[0]).then_inc(c_in, 16)
            for n, w in enumerate((q_proj, k_proj, v_proj, o_proj, g_w, out_w)):
                sp.dma_start(raw_w[:, n, :], w).then_inc(raw_in, 16)
            sp.wait_ge(raw_zero, 1)
            sp.dma_start(raw_w[0:E, 6, :], expert_sel).then_inc(raw_in, 16)
            for dst, w in ((wq2, W_Q), (wk2, W_K), (wv2, W_V)):
                sp.dma_start(dst[:, :].rearrange("d (h e) -> d h e", h=H),
                             w.rearrange("h d e -> d h e")).then_inc(w2_in, 16)
            sp.dma_start(gb[:, :], g_b.rearrange("(d a) -> d a", a=1)).then_inc(bias_in, 16)
            sp.dma_start(ob[:, :], out_b.rearrange("(a d) -> a d", a=1).broadcast_to([P, D])).then_inc(bias_in, 16)
            sp.dma_start(keys_sb[:, :, :], keys.rearrange("e d f -> d e f")).then_inc(experts_in, 16)
            sp.dma_start(vals_sb[:, :, :], values.rearrange("e f v -> (e f) v")
                         .rearrange("(b p) v -> p b v", p=P)).then_inc(experts_in, 16)

            def load_next(i):
                sp.wait_ge(pe_cT, i + 1)
                sp.dma_start(c_tok[:, :, :], ctx_tiles[i + 1]).then_inc(c_in, 16)
                sp.wait_ge(h1_set, i + 1)
                sp.dma_start(x_tok[:, :, :], x_tiles[i + 1]).then_inc(x_in, 16)

            def spread_gates(i):
                sp.wait_ge(gatesT_set, i + 1)
                for c in range(PAIRS):
                    sp.dma_start(gate_rows[:, c * P:(c + 1) * P],
                                 gatesT[c * E:(c + 1) * E, :]).then_inc(gates_out, 16)
                sp.wait_ge(gates_out, 64 * i + 64)
                rows = gate_rows.rearrange("(b two) t -> two b t", two=2)
                for half in range(2):
                    src = rows[half:half + 1].broadcast_to([F, BLOCKS, TOK])
                    sp.dma_start(gate_bc[F * half:F * half + F, :, :], src).then_inc(gates_in, 16)

            def store(f):
                sp.wait_ge(out_set, 4 * f + 4)
                sp.dma_start(out_tiles[f], out_tok[:, :, :]).then_inc(stored, 16)

            load_next(0)
            spread_gates(0)
            with sp.Fori(1, TILES - 1) as i:
                load_next(i)
                store(i - 1)
                spread_gates(i)
            store(TILES - 2)
            spread_gates(TILES - 1)
            store(TILES - 1)
            sp.wait_ge(stored, 16 * TILES + 16)

        @block.tensor
        def _(pe):
            mm, tr = nc.tensor.matmul, nc.tensor.transpose

            pe.wait_ge(consts_in, 16)
            pe.wait_ge(raw_in, 16 * 7)
            for n in range(7):
                tr(W[n // 4][:, (n % 4) * P:(n % 4 + 1) * P], raw_w[:, n, :], ident).then_inc(w_turned, 1)

            def turn(dst, tok):
                for c in range(PAIRS):
                    last = tr(dst[:, c * P:(c + 1) * P], tok[:, c, :], ident)
                return last

            def values_of(src, w, dst, g):
                for b in range(4):
                    s = src[:, (4 * g + b) * S:(4 * g + b + 1) * S]
                    for half in range(2):
                        last = mm(dst[half * S:(half + 1) * S, b * P:(b + 1) * P], s, w, start=True, stop=True)
                return last

            def weighted_values(u, pad, weights, done):
                for c2 in range(2):
                    for b in range(2):
                        seq = 4 * u + 2 * c2 + b
                        for e in range(2):
                            for r in range(QUADS):
                                last = mm(O[32 * r:32 * r + 32, seq * S:(seq + 1) * S],
                                          pad[:, seq // 4, (seq % 4) * 4 + r, 2 * e:2 * e + 2, :],
                                          weights(r, c2, b, e), start=(e == 0), stop=(e == 1))
                last.then_inc(done, 1)

            def expert_block(f, k):
                if k == 0:
                    pe.wait_ge(h3_set, f + 1)
                if k >= 2:
                    pe.wait_ge(hid_set, 16 * f + k - 1)
                mm(HB[k % 2][:, :], keys_sb[:, 2 * k:2 * k + 2, :], x2T[:, :],
                   start=True, stop=True).then_inc(pe_hid, 1)
                if k >= 1:
                    expert_out(f, k - 1)

            def expert_out(f, k):
                if k == 0:
                    pe.wait_ge(yT_set, f + 1)
                pe.wait_ge(hid_set, 16 * f + k + 1)
                mm(Y[:, :], vals_sb[:, k, :], hidden[k % 2][:, :],
                   start=(k == 0), stop=(k == BLOCKS - 1)).then_inc(pe_y, 1)

            def tile(i, attend, experts):
                f = i - 1

                def fill(key):
                    if experts:
                        for k in blocks_at(key):
                            expert_block(f, k)

                if attend:
                    pe.wait_ge(x_in, 16 * i + 16)
                    if experts:
                        pe.wait_ge(x2T_set, i)
                        pe.wait_ge(gatesT_set, i)
                        pe.wait_ge(sel_exp, i)
                    turn(W[0], x_tok).then_inc(pe_xT, 1)
                    pe.wait_ge(c_in, 16 * i + 16)
                    turn(W[1], c_tok).then_inc(pe_cT, 1)
                    pe.wait_ge(xT_set, i + 1)
                    if experts:
                        pe.wait_ge(h2_set, i)
                        pe.wait_ge(gated_set, i)
                    mm(W[2][:, :], wkT, xT[:, :], start=True, stop=True).then_inc(pe_k, 1)
                    mm(W[3][:, :], wqT, xT[:, :], start=True, stop=True).then_inc(pe_q, 1)
                    values_of(xT, wvT, W[0], 0).then_inc(pe_v, 1)
                    pe.wait_ge(cT_set, i + 1)
                    values_of(xT, wvT, W[1], 1).then_inc(pe_v, 1)
                fill("start")
                fill("after_v")
                if attend:
                    for u in range(UNITS):
                        if u == 0:
                            pe.wait_ge(kT_set, i + 1)
                            pe.wait_ge(qT_set, i + 1)
                            pe.wait_ge(v_set, 4 * i + 4)
                            pe.wait_ge(k_exp_set, 4 * i + 4)
                        else:
                            pe.wait_ge(probsT_set, 8 * i + 4)
                        for c2 in range(2):
                            for b in range(2):
                                t0 = ((2 * u + c2) * 2 + b) * S
                                for r in range(QUADS):
                                    rows = slice(32 * r, 32 * r + 32)
                                    last = mm(W[r][b * S:(b + 1) * S, c2 * 256:(c2 + 1) * 256],
                                              qT[rows, t0:t0 + S], k_exp[rows, :, t0:t0 + S],
                                              start=True, stop=True)
                        last.then_inc(pe_scores, 1)
                        fill(f"scores{u}")
                        for r in range(QUADS):
                            pe.wait_ge(exp_set, 8 * i + 4 * u + r + 1)
                            for n in range(4):
                                last = tr(W[r][:, n * P:(n + 1) * P], probs[r][:, n * P:(n + 1) * P], ident)
                            last.then_inc(pe_probsT, 1)
                        if u == 0 and experts:
                            pe.wait_ge(retT_set, i)
                        pe.wait_ge(probsT_set, 8 * i + 4 * u + 4)
                        weighted_values(u, v_pad[0], lambda r, c2, b, e: probsT[r][
                            :, (2 * c2 + e) * P + b * S:(2 * c2 + e) * P + (b + 1) * S], pe_attn)
                else:
                    fill("scores0")
                    fill("scores1")
                if attend:
                    pe.wait_ge(probsT_set, 8 * i + 8)
                    mm(W[1][:, :], wk2[:, :], cT[:, :], start=True, stop=True)
                    mm(W[2][:, :], wk2r[:, :], cT[:, :], start=True, stop=True).then_inc(pe_k2, 1)
                    pe.wait_ge(wide_set, i + 1)
                    for c in range(PAIRS):
                        last = tr(W[0][:, c * P:(c + 1) * P], inv_wide[:, c, :, :], ident)
                    last.then_inc(pe_inv, 1)
                fill("norm")
                if attend:
                    pe.wait_ge(attnT_set, i + 1)
                    for c in range(PAIRS):
                        last = mm(W[3][:, c * P:(c + 1) * P], attnT[:, c * P:(c + 1) * P], woT,
                                  start=True, stop=True)
                    last.then_inc(pe_o, 1)
                    pe.wait_ge(invT_set, i + 1)
                    values_of(cT, wv2[:, :], W[0], 0).then_inc(pe_v2, 1)
                    pe.wait_ge(k2_mul, 2 * i + 2)
                    values_of(cT, wv2[:, :], W[1], 1).then_inc(pe_v2, 1)
                fill("x1")
                if attend:
                    pe.wait_ge(x1_set, 4 * i + 4)
                    turn(W[2], x1_tok).then_inc(pe_x1T, 1)
                    pe.wait_ge(x1T_set, i + 1)
                    pe.wait_ge(v2_set, 4 * i + 4)
                    mm(W[0][:, :], wq2[:, :], x1T[:, :], start=True, stop=True)
                    mm(W[1][:, :], wq2r[:, :], x1T[:, :], start=True, stop=True).then_inc(pe_q2, 1)
                    mm(W[3][:, :], wgT, x1T[:, :], start=True, stop=True).then_inc(pe_gate, 1)
                fill("sim")
                if attend:
                    for u in range(UNITS):
                        if u == 0:
                            pe.wait_ge(q2_set, i + 1)
                            pe.wait_ge(k2_exp_set, 4 * i + 4)
                            pe.wait_ge(gate_set, i + 1)
                        else:
                            pe.wait_ge(decayed, 8 * i + 4)
                        for c2 in range(2):
                            for b in range(2):
                                seq = (2 * u + c2) * 2 + b
                                t0 = seq * S
                                for e in range(2):
                                    o0 = ((2 * c2 + b) * 2 + e) * S
                                    for r in range(QUADS):
                                        rows = slice(32 * r, 32 * r + 32)
                                        last = mm(W[r][:, o0:o0 + S],
                                                  k2_exp[rows, seq, 2 * e:2 * e + 2, :],
                                                  q2T[rows, t0:t0 + S], start=True, stop=True)
                        last.then_inc(pe_sim, 1)
                        pe.wait_ge(decayed, 8 * i + 4 * u + 4)
                        if u == 0:
                            pe.wait_ge(attnT_set, i + 1)
                        weighted_values(u, v_pad[1], lambda r, c2, b, e: simT[r][
                            :, ((2 * c2 + b) * 2 + e) * S:((2 * c2 + b) * 2 + e + 1) * S], pe_ret)
                fill("group")
                if attend:
                    pe.wait_ge(retT_set, i + 1)
                    mm(W[0][:, :], centre, retT[:, :], start=True, stop=True).then_inc(pe_cen, 1)
                fill("var")
                if attend:
                    pe.wait_ge(sq_set, i + 1)
                    mm(W[1][:, :], head_mean, sqT[:, :], start=True, stop=True).then_inc(pe_var, 1)
                fill("out")
                if experts:
                    expert_out(f, BLOCKS - 1)
                if attend:
                    pe.wait_ge(gated_set, i + 1)
                    for c in range(PAIRS):
                        last = mm(W[2][:, c * P:(c + 1) * P], gated[:, c * P:(c + 1) * P], wouT,
                                  start=True, stop=True)
                    last.then_inc(pe_out, 1)
                if experts:
                    pe.wait_ge(yT_set, f + 2)
                    for c in range(PAIRS):
                        last = tr(HB[0][:, c * P:(c + 1) * P], yT[:, c * P:(c + 1) * P], ident)
                    last.then_inc(pe_ytok, 1)
                if attend:
                    pe.wait_ge(x2_set, 4 * i + 4)
                    pe.wait_ge(cen_set, i + 1)
                    turn(W[0], x2_tok).then_inc(pe_x2T, 1)
                    pe.wait_ge(x2T_set, i + 1)
                    pe.wait_ge(gvar_set, i + 1)
                    for c in range(PAIRS):
                        last = mm(W[1][:, c * E:(c + 1) * E], x2T[:, c * P:(c + 1) * P], selT[:, 0:E],
                                  start=True, stop=True)
                    last.then_inc(pe_sel, 1)
                    pe.wait_ge(gates_set, i + 1)
                    tr(W[3][:, 0:P], gates[:, :, :], ident).then_inc(pe_gates, 1)

            pe.wait_ge(w_copied, 2)
            pe.wait_ge(w_rot, 4)
            pe.wait_ge(w2_in, 16 * 3)
            pe.wait_ge(experts_in, 16 * 2)
            over_tiles(pe, tile)

        @block.scalar
        def _(act):
            run = nc.scalar.activation
            for n in range(2):
                w = (4, 3)[n]
                act.wait_ge(w_turned, (4, 7)[n])
                run(wT[:, 4 * n:4 * n + w, :], W[n][:, 0:w * P], ACT.Copy).then_inc(w_copied, 1)
            act.wait_ge(bias_in, 32)
            run(gb_neg[:, :], gb[:, :], ACT.Copy, scale=-1.0).then_inc(w_copied, 1)
            act.wait_ge(w_copied, 3)
            act.sem_inc(yT_set, 1)
            act.wait_ge(pads_set, 2)

            def values_out(bank, pad, done, g):
                for h2 in range(2):
                    rows, d = slice(64 * h2, 64 * h2 + 64), slice(HD * h2, HD * h2 + HD)
                    run(pad[rows, g, :, 0:4:3, d],
                        bank[rows, :].rearrange("p (n e d) -> p n e d", e=2, d=16)[:, :, :, d],
                        ACT.Copy).then_inc(done, 1)

            def root(mo, ln, rs, mo_s, ln_s, rs_s, mo_n, n):
                act.wait_ge(mo_s, mo_n)
                run(ln[:, :], mo[:, :, 1:2].rearrange("p c o -> p (c o)"), ACT.Ln, bias=eps).then_inc(ln_s, 1)
                act.wait_ge(ln_s, n)
                run(rs[:, :], ln[:, :], ACT.Exp, scale=-0.5).then_inc(rs_s, 1)

            def tile(i, attend, experts):
                f = i - 1
                if attend:
                    act.wait_ge(pe_xT, i + 1)
                    run(xT[:, :], W[0][:, :], ACT.Copy).then_inc(xT_set, 1)
                    act.wait_ge(pe_cT, i + 1)
                    run(cT[:, :], W[1][:, :], ACT.Copy).then_inc(cT_set, 1)
                    act.wait_ge(pe_k, i + 1)
                    run(kT[:, :], W[2][:, :], ACT.Copy).then_inc(kT_set, 1)
                    act.wait_ge(pe_q, i + 1)
                    run(qT[:, :], W[3][:, :], ACT.Copy).then_inc(qT_set, 1)
                    for g in range(2):
                        act.wait_ge(pe_v, 2 * i + g + 1)
                        values_out(W[g], v_pad[0], v_set, g)
                    for u in range(UNITS):
                        for r in range(QUADS):
                            act.wait_ge(shifted, 8 * i + 4 * u + r + 1)
                            run(probs[r][:, :], probs[r][:, :], ACT.Exp, scale=SCALE).then_inc(exp_set, 1)
                        for r in range(QUADS):
                            act.wait_ge(pe_probsT, 8 * i + 4 * u + r + 1)
                            run(probsT[r][:, :], W[r][:, :], ACT.Copy).then_inc(probsT_set, 1)
                    act.wait_ge(pe_inv, i + 1)
                    run(invT[:, :], W[0][:, :], ACT.Copy).then_inc(invT_set, 1)
                    for g in range(2):
                        act.wait_ge(pe_v2, 2 * i + g + 1)
                        values_out(W[g], v_pad[1], v2_set, g)
                    root(moments, var_ln, rstd, mo_set, ln_set, rs_set, 8 * i + 4, 2 * i + 1)
                    act.wait_ge(pe_x1T, i + 1)
                    run(x1T[:, :], W[2][:, :], ACT.Copy).then_inc(x1T_set, 1)
                    act.wait_ge(pe_gate, i + 1)
                    run(swish[:, :], W[3][:, :], ACT.Exp, scale=-1.0, bias=gb_neg[:, :]).then_inc(sw_exp, 1)
                    act.wait_ge(pe_ret, 2 * i + 2)
                    run(retT[:, :], O[:, :], ACT.Copy).then_inc(retT_set, 1)
                    act.wait_ge(pe_cen, i + 1)
                    run(cenT[:, :], W[0][:, :], ACT.Copy).then_inc(cen_set, 1)
                    act.wait_ge(cen_set, i + 1)
                    run(sqT[:, :], cenT[:, :], ACT.Square).then_inc(sq_set, 1)
                    act.wait_ge(pe_var, i + 1)
                    run(gvar[:, :], W[1][:, :], ACT.Ln, bias=eps).then_inc(gvar_set, 1)
                    act.wait_ge(gvar_set, i + 1)
                    run(grs[:, :], gvar[:, :], ACT.Exp, scale=-0.5).then_inc(grs_set, 1)
                if experts:
                    act.wait_ge(pe_y, 16 * f + 16)
                    run(yT[:, :], Y[:, :], ACT.Copy).then_inc(yT_set, 1)
                if attend:
                    root(moments, var_ln, rstd, mo_set, ln_set, rs_set, 8 * i + 8, 2 * i + 2)
                if experts:
                    root(moments3, var_ln3, rstd3, mo3_set, ln3_set, rs3_set, 4 * f + 4, f + 1)
                if attend:
                    act.wait_ge(pe_x2T, i + 1)
                    run(x2T[:, :], W[0][:, :], ACT.Copy).then_inc(x2T_set, 1)
                    act.wait_ge(pe_sel, i + 1)
                    run(sel_e[:, :, :], W[1][:, 0:PAIRS * E], ACT.Exp, scale=-1.0).then_inc(sel_exp, 1)
                    act.wait_ge(pe_gates, i + 1)
                    if experts:
                        act.wait_ge(gates_out, 64 * i)
                    run(gatesT[:, :], W[3][:, 0:P], ACT.Copy).then_inc(gatesT_set, 1)

            over_tiles(act, tile)

        @block.vector
        def _(dve):
            v = nc.vector
            v.memset(raw_w[:, 6, :], 0.0).then_inc(raw_zero, 1)
            v.memset(sel_g[:, :, E:E + MAX8 - TOP], -1.0).then_inc(zeros_set, 1)
            v.memset(tops[:, :, :], -1.0).then_inc(zeros_set, 1)
            dve.wait_ge(zeros_set, 2)
            dve.wait_ge(w2_in, 16 * 3)
            for w, wr in ((wq2, wq2r), (wk2, wk2r)):
                a = w[:, :].rearrange("p (n two) -> p n two", two=2)
                b = wr[:, :].rearrange("p (n two) -> p n two", two=2)
                v.tensor_scalar(b[:, :, 0:1], a[:, :, 1:2], -1.0, None, ALU.mult).then_inc(w_rot, 1)
                v.tensor_copy(b[:, :, 1:2], a[:, :, 0:1]).then_inc(w_rot, 1)
            dve.wait_ge(consts_in, 16)
            dve.sem_inc(h3_set, 1)

            def norm(n, h, st, mo, rs, dst, st_s, mo_s, rs_s, dst_s, base, rs_base, dst_base):
                for c in range(PAIRS):
                    v.bn_stats(st[:, c, :], h[:, c, :]).then_inc(st_s, 1)
                dve.wait_ge(st_s, base + PAIRS)
                v.memset(spare[:, :], 0.0)
                for c in range(PAIRS):
                    v.bn_aggr(mo[:, c, :], st[:, c, :]).then_inc(mo_s, 1)
                dve.wait_ge(mo_s, base + PAIRS)
                dve.wait_ge(rs_s, rs_base + 1)
                for c in range(PAIRS):
                    v.tensor_scalar(dst[:, c, :], h[:, c, :], mo[:, c, 0:1], rs[:, c:c + 1],
                                    ALU.subtract, ALU.mult).then_inc(dst_s, 1)

            def gate_block(f, k):
                if k == 0:
                    dve.wait_ge(gates_in, 32 * f + 32)
                dve.wait_ge(pe_hid, 16 * f + k + 1)
                if k >= 2:
                    dve.wait_ge(pe_y, 16 * f + k - 1)
                v.scalar_tensor_tensor(out=hidden[k % 2][:, :], in0=HB[k % 2][:, :], scalar=0.0,
                                       in1=gate_bc[:, k, :], op0=ALU.max, op1=ALU.mult).then_inc(hid_set, 1)

            def over_seqs(ap):
                return ap.rearrange("p (a t) -> p a t", a=1).broadcast_to([P, SEQS, S])

            def seqs(ap):
                return ap.rearrange("p (a t) -> p a t", t=S)

            def tile(i, attend, experts):
                f = i - 1

                def fill(key):
                    if experts:
                        for k in blocks_at(key):
                            gate_block(f, k)

                fill("start")
                fill("after_v")
                for u in range(UNITS):
                    if attend:
                        dve.wait_ge(pe_scores, 2 * i + u + 1)
                        for r in range(QUADS):
                            if u == 1:
                                dve.wait_ge(sum_set, 8 * i + r + 1)
                                dve.wait_ge(pe_probsT, 8 * i + r + 1)
                            v.tensor_tensor(probs[r][:, :].rearrange("p (a t) -> p a t", t=S),
                                            W[r][:, :].rearrange("p (a t) -> p a t", t=S),
                                            over_seqs(causal), ALU.add).then_inc(masked, 1)
                            dve.wait_ge(masked, 8 * i + 4 * u + r + 1)
                            v.tensor_reduce(row_max[:, r, :], probs[r][:, :].rearrange("p (a t) -> p a t", t=S),
                                            axis=AX.X, op=ALU.max).then_inc(max_set, 1)
                    fill(f"scores{u}")
                    if attend:
                        for r in range(QUADS):
                            dve.wait_ge(exp_set, 8 * i + 4 * u + r + 1)
                            v.tensor_reduce(row_sum[:, 2 * u:2 * u + 2, r, :],
                                            probs[r][:, :].rearrange("p (c j t) -> p c j t", c=2, t=S),
                                            axis=AX.X, op=ALU.add).then_inc(sum_set, 1)
                if attend:
                    dve.wait_ge(sum_set, 8 * i + 8)
                    v.reciprocal(row_inv[:, :, :], row_sum[:, :, :, :].rearrange("p c r j -> p c (r j)")).then_inc(inv_set, 1)
                    dve.wait_ge(pe_k2, i + 1)
                    v.tensor_tensor(seqs(k2c[:, :]), seqs(W[1][:, :]), over_seqs(k_cos), ALU.mult).then_inc(k2_mul, 1)
                    v.tensor_tensor(seqs(k2s[:, :]), seqs(W[2][:, :]), over_seqs(k_sin), ALU.mult).then_inc(k2_mul, 1)
                    dve.wait_ge(invT_set, i + 1)
                    dve.wait_ge(pe_attn, 2 * i + 2)
                    v.tensor_tensor(attnT[:, :], O[:, :], invT[:, :], ALU.mult).then_inc(attnT_set, 1)
                fill("norm")
                if attend:
                    dve.wait_ge(pe_o, i + 1)
                    v.tensor_tensor(h_tok[:, :, :], W[3][:, :].rearrange("p (c d) -> p c d", c=PAIRS),
                                    x_tok[:, :, :], ALU.add).then_inc(h1_set, 1)
                    dve.wait_ge(h1_set, i + 1)
                    norm(0, h_tok, stats, moments, rstd, x1_tok, st_set, mo_set, rs_set, x1_set,
                         8 * i, 2 * i, 4 * i)
                fill("x1")
                if attend:
                    dve.wait_ge(pe_q2, i + 1)
                    v.tensor_tensor(seqs(q2c[:, :]), seqs(W[0][:, :]), over_seqs(q_cos), ALU.mult).then_inc(q2_mul, 1)
                    v.tensor_tensor(seqs(q2s[:, :]), seqs(W[1][:, :]), over_seqs(q_sin), ALU.mult).then_inc(q2_mul, 1)
                    dve.wait_ge(sw_exp, i + 1)
                    v.tensor_scalar(swish_d[:, :], swish[:, :], 1.0, None, ALU.add).then_inc(sw_add, 1)
                    dve.wait_ge(sw_add, i + 1)
                    v.reciprocal(sw_rec[:, :], swish_d[:, :]).then_inc(sw_inv, 1)
                    dve.wait_ge(sw_inv, i + 1)
                    v.scalar_tensor_tensor(out=gateT[:, :], in0=W[3][:, :], scalar=gb[:, :], in1=sw_rec[:, :],
                                           op0=ALU.add, op1=ALU.mult).then_inc(gate_set, 1)
                fill("sim")
                if attend:
                    for u in range(UNITS):
                        dve.wait_ge(pe_sim, 2 * i + u + 1)
                        if u == 1:
                            dve.wait_ge(pe_ret, 2 * i + 1)
                        for r in range(QUADS):
                            table = decay[:, 2 * r * S:(2 * r + 2) * S].rearrange("p (a t) -> p a t", a=1)
                            v.tensor_tensor(simT[r][:, :].rearrange("p (a t) -> p a t", a=4),
                                            W[r][:, :].rearrange("p (a t) -> p a t", a=4),
                                            table.broadcast_to([P, 4, P]), ALU.mult).then_inc(decayed, 1)
                fill("group")
                fill("var")
                if attend:
                    pass
                fill("out")
                if attend:
                    dve.wait_ge(pe_out, i + 1)
                    dve.wait_ge(x1b_set, i + 1)
                    dve.wait_ge(x1_set, 4 * i + 4)
                    v.tensor_tensor(h_tok[:, :, :], W[2][:, :].rearrange("p (c d) -> p c d", c=PAIRS),
                                    x1b_tok[:, :, :], ALU.add).then_inc(h2_set, 1)
                if experts:
                    dve.wait_ge(pe_ytok, f + 1)
                    v.tensor_tensor(h3_tok[:, :, :], HB[0][:, :].rearrange("p (c d) -> p c d", c=PAIRS),
                                    x2_tok[:, :, :], ALU.add).then_inc(h3_set, 1)
                if attend:
                    dve.wait_ge(h2_set, i + 1)
                    if experts:
                        dve.wait_ge(h3_set, i + 1)
                    norm(1, h_tok, stats, moments, rstd, x2_tok, st_set, mo_set, rs_set, x2_set,
                         8 * i + 4, 2 * i + 1, 4 * i)
                if experts:
                    dve.wait_ge(h3_set, f + 2)
                    dve.wait_ge(stored, 16 * f + 16)
                    norm(2, h3_tok, stats3, moments3, rstd3, out_tok, st3_set, mo3_set, rs3_set, out_set,
                         4 * f, f, 4 * f)
                if attend:
                    dve.wait_ge(sel_exp, i + 1)
                    v.tensor_scalar(sel_d[:, :, :], sel_e[:, :, :], 1.0, None, ALU.add).then_inc(sel_add, 1)
                    dve.wait_ge(sel_add, i + 1)
                    v.reciprocal(sel_g[:, :, 0:E], sel_d[:, :, :]).then_inc(sel_inv, 1)
                    wait_apart(dve, zeros_set, 2, sel_inv, i + 1)
                    for c in range(PAIRS):
                        v.max(tops[:, c, :], sel_g[:, c, 0:E]).then_inc(top_set, 1)
                    dve.wait_ge(top_set, 4 * i + 4)
                    v.memset(tops[:, :, TOP:MAX8], -1.0).then_inc(top_cut, 1)
                    wait_apart(dve, zeros_set, 2, top_cut, i + 1)
                    for c in range(PAIRS):
                        v.match_replace(out=sel_m[:, c, :], in_to_replace=tops[:, c, :],
                                        in_values=sel_g[:, c, :], imm_value=0.0).then_inc(matched, 1)
                    dve.wait_ge(matched, 4 * i + 4)
                    v.tensor_tensor(gates[:, :, :], sel_g[:, :, 0:E], sel_m[:, :, 0:E],
                                    ALU.subtract).then_inc(gates_set, 1)

            over_tiles(dve, tile)

        @block.gpsimd
        def _(pool):
            g = nc.gpsimd
            for a in range(2):
                g.memset(v_pad[a][:, :, :, :, :], 0.0).then_inc(pads_set, 1)
            pool.wait_ge(consts_in, 16)

            def tile(i, attend, experts):
                f = i - 1
                if attend:
                    pool.wait_ge(kT_set, i + 1)
                    g.tensor_tensor(k_exp[:, 0, :], kT[:, :], head_pick[:, 0:1].broadcast_to([P, TOK]),
                                    ALU.mult).then_inc(k_exp_set, 1)
                    for j in range(1, 4):
                        g.tensor_scalar(k_exp[:, j, :], kT[:, :], head_pick[:, j:j + 1], None,
                                        ALU.mult).then_inc(k_exp_set, 1)
                    for u in range(UNITS):
                        for r in range(QUADS):
                            pool.wait_ge(max_set, 8 * i + 4 * u + r + 1)
                            top = row_max[:, r, :].rearrange("p (a o) -> p a o", o=1).broadcast_to([P, 8, S])
                            s = probs[r][:, :].rearrange("p (a t) -> p a t", t=S)
                            g.tensor_tensor(s, s, top, ALU.subtract).then_inc(shifted, 1)
                    wait_apart(pool, bias_in, 32, inv_set, i + 1)
                    wide = row_inv[:, :, :].rearrange("p c h -> p (c h)").rearrange("p (a o) -> p a o", o=1)
                    g.tensor_copy(inv_wide[:, :, :, :].rearrange("p c h d -> p (c h) d"),
                                  wide.broadcast_to([P, PAIRS * H, HD])).then_inc(wide_set, 1)
                    pool.wait_ge(k2_mul, 2 * i + 2)
                    g.tensor_tensor(k2T[:, :], k2c[:, :], k2s[:, :], ALU.add).then_inc(k2_set, 1)
                    wait_apart(pool, bias_in, 32, k2_set, i + 1)
                    for j in range(4):
                        g.tensor_scalar(k2_exp[:, :, j, :], k2T[:, :].rearrange("p (a t) -> p a t", t=S), head_pick[:, j:j + 1], None,
                                        ALU.mult).then_inc(k2_exp_set, 1)
                    pool.wait_ge(q2_mul, 2 * i + 2)
                    g.tensor_tensor(q2T[:, :], q2c[:, :], q2s[:, :], ALU.add).then_inc(q2_set, 1)
                    pool.wait_ge(x1_set, 4 * i + 4)
                    g.tensor_tensor(x1b_tok[:, :, :], x1_tok[:, :, :],
                                    ob[:, :].rearrange("p (a d) -> p a d", a=1).broadcast_to([P, PAIRS, D]),
                                    ALU.add).then_inc(x1b_set, 1)
                    pool.wait_ge(grs_set, i + 1)
                    pool.wait_ge(gate_set, i + 1)
                    g.tensor_tensor(ggate[:, :], grs[:, :], gateT[:, :], ALU.mult).then_inc(ggate_set, 1)
                    pool.wait_ge(ggate_set, i + 1)
                    pool.wait_ge(cen_set, i + 1)
                    g.tensor_tensor(gated[:, :], cenT[:, :], ggate[:, :], ALU.mult).then_inc(gated_set, 1)

            pool.wait_ge(bias_in, 32)
            over_tiles(pool, tile)


def constant_table():
    import numpy as np
    P, S, H, HD, QUAD = 128, 64, 16, 8, 4
    p = np.arange(P)
    same_head = (p[:, None] // HD == p[None, :] // HD) / HD
    causal = np.where(np.arange(S)[None, :] <= (p % S)[:, None], 0.0, -3.0e38)
    f4 = np.float32
    gammas = (1.0 - np.exp(np.linspace(np.log(1.0 / 32.0), np.log(1.0 / 512.0), H).astype(f4))).astype(f4)
    dist = np.arange(S)[None, None, :] - (p % S)[:, None, None]
    head = 2 * np.arange(H // 2)[None, :, None] + (p // S)[:, None, None]
    decay = np.where(dist >= 0, gammas[head].astype(np.float64) ** np.maximum(dist, 0), 0.0)
    base = ((np.arange(0, HD, 2) + 0.4 * HD) / (1.4 * HD)).astype(f4).astype(np.float64)
    power = np.arange(-(S // 2), S - S // 2) / 512.0
    scale = base[None, :] ** power[:, None]
    inv_freq = (1.0 / 10000.0 ** (np.arange(HD // 2, dtype=f4) / f4(HD // 2))).astype(f4)
    ang = (np.arange(S, dtype=f4)[:, None] * inv_freq[None, :]).astype(np.float64)
    rows = (p % HD) // 2
    turns = [t[:, rows].T for t in (np.cos(ang) * scale, np.sin(ang) * scale,
                                    np.cos(ang) / scale, np.sin(ang) / scale)]
    pick = ((p // HD) % QUAD)[:, None] == np.arange(QUAD)[None, :]
    return np.ascontiguousarray(np.concatenate(
        [np.eye(P), np.eye(P) - same_head, same_head, causal, decay.reshape(P, -1), *turns, pick,
         np.full((P, 1), 1e-5)], axis=1).astype(f4))


_INS = ["x", "ctx_1024", "L0_attn_q_proj", "L0_attn_k_proj", "L0_attn_v_proj", "L0_attn_o_proj",
        "L0_xattn_W_Q", "L0_xattn_W_K", "L0_xattn_W_V", "L0_xattn_g_w", "L0_xattn_g_b",
        "L0_xattn_out_w", "L0_xattn_out_b", "L0_ffn_expert_sel", "L0_ffn_keys", "L0_ffn_values"]


def kernel(**inputs):
    import numpy as np
    import concourse.bacc as bacc
    from concourse import mybir
    from concourse.bass_utils import run_bass_kernel_spmd as run

    nc = bacc.Bacc("TRN2", target_bir_lowering=False, num_devices=1)
    arrays, args = {}, []
    named = [(name, np.ascontiguousarray(inputs[name])) for name in _INS] + [("consts", constant_table())]
    for name, a in named:
        arrays[f"in_{name}"] = a
        args.append(nc.dram_tensor(f"in_{name}", a.shape, mybir.dt.from_np(a.dtype), kind="ExternalInput").ap())
    args.append(nc.dram_tensor("out_0", inputs["x"].shape, mybir.dt.float32, kind="ExternalOutput").ap())
    decoder_layer(nc, *args)
    r = run(nc, [arrays], core_ids=[0])
    return r.results[0]["out_0"]
```

```python
import concourse.bass as bass
from concourse import mybir
from contextlib import ExitStack


def decoder_layer(nc: bass.Bass, x, ctx_in, q_proj, k_proj, v_proj, o_proj, W_Q, W_K, W_V, g_w, g_b,
                  out_w, out_b, expert_sel, keys, values, consts, out):
    f32 = mybir.dt.float32
    ALU = mybir.AluOpType
    ACT = mybir.ActivationFunctionType
    AX = mybir.AxisListType

    BATCH, S, D = x.shape
    H, _, HD = W_Q.shape
    E, _, F = keys.shape
    P = 128
    TOK = 512
    TILES = BATCH * S // TOK
    PAIRS = TOK // P
    SEQS = TOK // S
    QUADS = 4
    BLOCKS = E * F // P
    TOP = 4
    GATE_PARTS = (0, 2, 4, 8)
    MAX8 = 8
    SCALE = float(HD) ** -0.5

    x_tiles = x.rearrange("b s d -> (b s) d").rearrange("(t c p) d -> t p c d", c=PAIRS, p=P)
    ctx_tiles = ctx_in.rearrange("b s d -> (b s) d").rearrange("(t c p) d -> t p c d", c=PAIRS, p=P)
    out_tiles = out.rearrange("b s d -> (b s) d").rearrange("(t c p) d -> t p c d", c=PAIRS, p=P)
    gate_rows = nc.dram_tensor("gate_rows", (E, TOK), f32, kind="Internal").ap()

    stack = ExitStack()
    with stack:
        def sb(name, shape):
            return stack.enter_context(nc.sbuf_tensor(name, shape, f32))

        def ps(name):
            return stack.enter_context(nc.psum_tensor(name, [P, 512], f32))

        def sem(name):
            return stack.enter_context(nc.semaphore(name))

        const = sb("const", [P, consts.shape[1]])
        col = [0]

        def part(n):
            col[0] += n
            return const[:, col[0] - n:col[0]]

        ident = part(P)
        head_mean = part(P)
        causal = part(S)
        decay = part(H * S)
        q_cos, q_sin, k_cos, k_sin = part(S), part(S), part(S), part(S)
        head_pick = part(8)
        eps = part(1)
        one = part(1)

        raw_w = sb("raw_w", [P, 7, P])
        wT = sb("wT", [P, 7, P])
        wqT, wkT, wvT, woT, wgT, wouT, selT = (wT[:, n, :] for n in range(7))
        wq2, wk2, wv2 = sb("wq2", [P, P]), sb("wk2", [P, P]), sb("wv2", [P, P])
        wq2r, wk2r = sb("wq2r", [P, P]), sb("wk2r", [P, P])
        wv2c = sb("wv2c", [P, P])
        head_sum = sb("head_sum", [P, 2, H])
        keys_sb = sb("keys_sb", [P, E, F])
        vals_sb = sb("vals_sb", [P, BLOCKS, P])
        gb, gb_neg = sb("gb", [P, 1]), sb("gb_neg", [P, 1])
        ob = sb("ob", [P, P])

        x_tok, xT = sb("x_tok", [P, PAIRS, D]), sb("xT", [P, TOK])
        xr_tok = sb("xr_tok", [P, PAIRS, D])
        qT, kT = sb("qT", [P, TOK]), sb("kT", [P, TOK])
        k_exp = sb("k_exp", [P, 2, 8, P])
        v_pad = sb("v_pad", [P, 2, PAIRS * QUADS, 4, 16])
        probs = [sb(f"probs{g}", [P, 512]) for g in range(2)]
        probsT = [sb(f"probsT{g}", [P, 512]) for g in range(2)]
        row_max = sb("row_max", [P, 2, 8])
        row_sum = sb("row_sum", [P, PAIRS, 2, 8])
        row_inv = sb("row_inv", [P, PAIRS, H])
        inv_wide = sb("inv_wide", [P, PAIRS, H, HD])
        rawT, attnT = sb("rawT", [P, TOK]), sb("attnT", [P, TOK])
        x1_tok, x1T = sb("x1_tok", [P, PAIRS, D]), sb("x1T", [P, TOK])
        c_tok, cT = sb("c_tok", [P, PAIRS, D]), sb("cT", [P, TOK])
        x1b_tok = sb("x1b_tok", [P, PAIRS, D])
        k2c, k2s, q2c, q2s = sb("k2c", [P, TOK]), sb("k2s", [P, TOK]), sb("q2c", [P, TOK]), sb("q2s", [P, TOK])
        k2T, q2T = sb("k2T", [P, TOK]), sb("q2T", [P, TOK])
        q2_exp = sb("q2_exp", [P, 2, 8, P])
        v2_pad = sb("v2_pad", [P, PAIRS, QUADS, 4 * 72])
        simT = [sb(f"simT{g}", [P, 512]) for g in range(2)]
        sw_e, sw_l, sw_r, gateT = sb("sw_e", [P, TOK]), sb("sw_l", [P, TOK]), sb("sw_r", [P, TOK]), sb("gateT", [P, TOK])
        ret_sep, ret_sq = sb("ret_sep", [P, TOK]), sb("ret_sq", [P, TOK])
        gvar, grs, retT, gated = sb("gvar", [P, TOK]), sb("grs", [P, TOK]), sb("retT", [P, TOK]), sb("gated", [P, TOK])
        x2_tok, x2T = sb("x2_tok", [P, PAIRS, D]), sb("x2T", [P, TOK])
        sel_e, sel_d = sb("sel_e", [P, PAIRS, E]), sb("sel_d", [P, PAIRS, E])
        sel_g = sb("sel_g", [P, PAIRS, E + MAX8 - TOP])
        sel_m = sb("sel_m", [P, PAIRS, E + MAX8 - TOP])
        tops = sb("tops", [P, PAIRS, MAX8])
        gates, gatesT = sb("gates", [P, PAIRS, E]), sb("gatesT", [P, P])
        gate_bc = sb("gate_bc", [P, BLOCKS, TOK])
        x2c_tok = sb("x2c_tok", [P, PAIRS, D])
        hidden = [sb(f"hidden{n}", [P, TOK]) for n in range(2)]
        yT, out_tok = sb("yT", [P, TOK]), sb("out_tok", [P, PAIRS, D])
        h_tok = [sb(f"h{n}_tok", [P, PAIRS, D]) for n in range(3)]
        stats = [sb(f"stats{n}", [P, PAIRS, 6]) for n in range(3)]
        moments = [sb(f"moments{n}", [P, PAIRS, 2]) for n in range(3)]
        var_ln = [sb(f"var_ln{n}", [P, PAIRS]) for n in range(3)]
        rstd = [sb(f"rstd{n}", [P, PAIRS]) for n in range(3)]
        spare = sb("spare", [P, 1])

        A = [ps("attn0"), ps("attn1")]
        R = [ps("ret0"), ps("ret1")]
        M = ps("third")
        HB = [ps("hid0"), ps("hid1")]
        Y = ps("expert_sum")

        consts_in, raw_in, w2_in, experts_in, bias_in = (sem(n) for n in (
            "consts_in", "raw_in", "w2_in", "experts_in", "bias_in"))
        zeros_set, raw_zero, pads_set = sem("zeros_set"), sem("raw_zero"), sem("pads_set")
        w_turned, w_copied, w_rot, w_mean = sem("w_turned"), sem("w_copied"), sem("w_rot"), sem("w_mean")
        xr_set = sem("xr_set")
        x_in, c_in = sem("x_in"), sem("c_in")
        pe_xT, pe_k, pe_q, xT_set, kT_set, qT_set = (sem(n) for n in (
            "pe_xT", "pe_k", "pe_q", "xT_set", "kT_set", "qT_set"))
        pe_v, v_set, k_exp_set = sem("pe_v"), sem("v_set"), sem("k_exp_set")
        pe_scores = sem("pe_scores")
        masked, max_set, shifted, exp_set, sum_set, pe_probsT, probsT_set = (sem(n) for n in (
            "masked", "max_set", "shifted", "exp_set", "sum_set", "pe_probsT", "probsT_set"))
        pe_attn, raw_set = sem("pe_attn"), sem("raw_set")
        inv_set, wide_set, pe_inv, attnT_set, pe_o, pe_x1T, x1T_set = (sem(n) for n in (
            "inv_set", "wide_set", "pe_inv", "attnT_set", "pe_o", "pe_x1T", "x1T_set"))
        pe_cT, cT_set, x1b_set, pe_k2, k2_set, pe_q2, q2_set = (sem(n) for n in (
            "pe_cT", "cT_set", "x1b_set", "pe_k2", "k2_set", "pe_q2", "q2_set"))
        k2_mul, q2_mul, q2_exp_set, pe_v2, v2_set = (sem(n) for n in (
            "k2_mul", "q2_mul", "q2_exp_set", "pe_v2", "v2_set"))
        pe_gate, sw_exp, sw_log, sw_inv, gate_set = (sem(n) for n in (
            "pe_gate", "sw_exp", "sw_log", "sw_inv", "gate_set"))
        pe_sim, decayed, pe_ret, ret_set = (sem(n) for n in (
            "pe_sim", "decayed", "pe_ret", "ret_set"))
        sq_set, pe_var, gvar_set, grs_set, retT_set, gated_set = (sem(n) for n in (
            "sq_set", "pe_var", "gvar_set", "grs_set", "retT_set", "gated_set"))
        pe_out, pe_x2T, x2T_set, pe_sel, sel_exp, sel_add, sel_inv = (sem(n) for n in (
            "pe_out", "pe_x2T", "x2T_set", "pe_sel", "sel_exp", "sel_add", "sel_inv"))
        top_set, top_cut, matched, gates_set, pe_gates, gatesT_set = (sem(n) for n in (
            "top_set", "top_cut", "matched", "gates_set", "pe_gates", "gatesT_set"))
        gates_out = sem("gates_out")
        gates_in = [sem(f"gates_in{n}") for n in range(len(GATE_PARTS))]
        x2c_set, pe_hid, hid_set, pe_y, yT_set, pe_ytok = (sem(n) for n in (
            "x2c_set", "pe_hid", "hid_set", "pe_y", "yT_set", "pe_ytok"))
        h_set = [sem(f"h{n}_set") for n in range(3)]
        st_set, mo_set = [sem(f"st{n}_set") for n in range(3)], [sem(f"mo{n}_set") for n in range(3)]
        ln_set, rs_set = [sem(f"ln{n}_set") for n in range(3)], [sem(f"rs{n}_set") for n in range(3)]
        x1_set, x2_set, out_set = sem("x1_set"), sem("x2_set"), sem("out_set")
        stored = sem("stored")

        block = stack.enter_context(nc.Block())

        def over_tiles(engine, turn):
            turn(0, None, None, None)
            turn(1, 0, None, None)
            turn(2, 1, 0, None)
            with engine.Fori(3, TILES) as i:
                turn(i, i - 1, i - 2, i - 3)
            turn(None, TILES - 1, TILES - 2, TILES - 3)
            turn(None, None, TILES - 1, TILES - 2)
            turn(None, None, None, TILES - 1)

        def after(engine, semaphore, value):
            if not isinstance(value, int) or value > 0:
                engine.wait_ge(semaphore, value)

        def wait_apart(engine, fixed, count, semaphore, value):
            engine.wait_ge(fixed, count)
            engine.wait_ge(semaphore, value)

        FILL = [("pair0", "scores", 0), ("pair0", "sims", 0), ("pair0", "ret", 0), ("pair0", "weighted", 2),
                ("pair1", "scores", 1), ("pair1", "sims", 1), ("pair1", "ret", 1), ("pair1", "weighted", 0),
                ("pair2", "scores", 1), ("pair2", "sims", 1), ("pair2", "ret", 1), ("pair2", "weighted", 1),
                ("pair3", "scores", 1), ("pair3", "sims", 1), ("pair3", "ret", 1), ("pair3", "weighted", 0),
                ("joint", "begin", 1), ("joint", "inverse", 1), ("joint", "project", 1), ("joint", "variance", 1)]
        assert sum(n for _, _, n in FILL) == BLOCKS

        def blocks_at(part_, step):
            at = 0
            for p_, s_, n in FILL:
                if (p_, s_) == (part_, step):
                    return range(at, at + n)
                at += n

        @block.sync
        def _(sp):
            sp.sem_inc(stored, 16)
            sp.dma_start(const[:, :], consts).then_inc(consts_in, 16)
            sp.dma_start(x_tok[:, :, :], x_tiles[0]).then_inc(x_in, 16)
            for n, w in enumerate((q_proj, k_proj, v_proj, o_proj, g_w, out_w)):
                sp.dma_start(raw_w[:, n, :], w).then_inc(raw_in, 16)
            sp.wait_ge(raw_zero, 1)
            sp.dma_start(raw_w[0:E, 6, :], expert_sel).then_inc(raw_in, 16)
            for dst, w in ((wq2, W_Q), (wk2, W_K), (wv2, W_V)):
                sp.dma_start(dst[:, :].rearrange("d (h e) -> d h e", h=H),
                             w.rearrange("h d e -> d h e")).then_inc(w2_in, 16)
            sp.dma_start(gb[:, :], g_b.rearrange("(d a) -> d a", a=1)).then_inc(bias_in, 16)
            sp.dma_start(ob[:, :], out_b.rearrange("(a d) -> a d", a=1).broadcast_to([P, D])).then_inc(bias_in, 16)
            sp.dma_start(c_tok[:, :, :], ctx_tiles[0]).then_inc(c_in, 16)
            sp.dma_start(keys_sb[:, :, :], keys.rearrange("e d f -> d e f")).then_inc(experts_in, 16)
            sp.dma_start(vals_sb[:, :, :], values.rearrange("e f v -> (e f) v")
                         .rearrange("(b p) v -> p b v", p=P)).then_inc(experts_in, 16)

            def turn(a, t, f, g, more_x=True, more_c=True):
                if t is not None and more_c:
                    sp.wait_ge(pe_cT, t + 1)
                    sp.dma_start(c_tok[:, :, :], ctx_tiles[t + 1]).then_inc(c_in, 16)
                if a is not None and more_x:
                    sp.wait_ge(pe_xT, a + 1)
                    sp.wait_ge(xr_set, a + 1)
                    sp.dma_start(x_tok[:, :, :], x_tiles[a + 1]).then_inc(x_in, 16)
                if f is not None:
                    sp.wait_ge(gatesT_set, f + 1)
                    sp.dma_start(gate_rows.rearrange("e (c p) -> c e p", c=PAIRS),
                                 gatesT[:, :]).then_inc(gates_out, 16)
                    sp.wait_ge(gates_out, 16 * f + 16)
                    rows = gate_rows.rearrange("(b two) t -> two b t", two=2)
                    for n, k in enumerate(GATE_PARTS):
                        end = (GATE_PARTS + (BLOCKS,))[n + 1]
                        for half in range(2):
                            sp.dma_start(gate_bc[F * half:F * half + F, k:end, :],
                                         rows[half:half + 1, k:end].broadcast_to([F, end - k, TOK])
                                         ).then_inc(gates_in[n], 16)
                if g is not None:
                    sp.wait_ge(out_set, 4 * g + 4)
                    sp.dma_start(out_tiles[g], out_tok[:, :, :]).then_inc(stored, 16)

            turn(0, None, None, None)
            turn(1, 0, None, None)
            turn(2, 1, 0, None)
            with sp.Fori(3, TILES - 1) as i:
                turn(i, i - 1, i - 2, i - 3)
            turn(TILES - 1, TILES - 2, TILES - 3, TILES - 4, more_x=False)
            turn(None, TILES - 1, TILES - 2, TILES - 3, more_c=False)
            turn(None, None, TILES - 1, TILES - 2)
            turn(None, None, None, TILES - 1)
            sp.wait_ge(stored, 16 * TILES + 16)

        @block.tensor
        def _(pe):
            mm, tr = nc.tensor.matmul, nc.tensor.transpose

            pe.wait_ge(consts_in, 16)
            pe.wait_ge(raw_in, 16 * 7)
            for n in range(7):
                tr(A[n // 4][:, (n % 4) * P:(n % 4 + 1) * P], raw_w[:, n, :], ident).then_inc(w_turned, 1)

            def turned(dst, tok):
                for c in range(PAIRS):
                    last = tr(dst[:, c * P:(c + 1) * P], tok[:, c, :], ident)
                return last

            def token_values(src, w, dst):
                for c in range(PAIRS):
                    last = mm(dst[:, c * P:(c + 1) * P], src[:, c * P:(c + 1) * P], w, start=True, stop=True)
                return last

            def weighted_values(p, weights, dst):
                for b in range(2):
                    for e in range(2):
                        for q in range(QUADS):
                            last = mm(dst[32 * q:32 * q + 32, b * S:(b + 1) * S],
                                      v_pad[:, b, p * QUADS + q, 2 * e:2 * e + 2, :],
                                      weights(b, 2 * q + e), start=(e == 0), stop=(e == 1))
                return last

            def retained_values(p, dst):
                for q in range(2):
                    for head in range(4):
                        for half in range(2):
                            last = mm(dst[64 * half:64 * half + 64, q * S:(q + 1) * S],
                                      v2_pad[:, p, 2 * half + q, head * 64:head * 64 + 64],
                                      simT[half][:, (4 * q + head) * S:(4 * q + head + 1) * S],
                                      start=(head == 0), stop=(head == 3))
                return last

            def hidden_of(f, k):
                if k == 0:
                    pe.wait_ge(h_set[2], f + 1)
                    pe.wait_ge(x2T_set, f + 1)
                if k == 1:
                    pe.wait_ge(gatesT_set, f + 1)
                if k >= 2:
                    pe.wait_ge(hid_set, 16 * f + k - 1)
                mm(HB[k % 2][:, :], keys_sb[:, 2 * k:2 * k + 2, :], x2T[:, :],
                   start=True, stop=True).then_inc(pe_hid, 1)

            def to_experts(f, k):
                if k >= 1:
                    hidden_of(f, k)
                    from_experts(f, k - 1)

            def from_experts(f, k):
                if k == 0:
                    pe.wait_ge(yT_set, f + 1)
                pe.wait_ge(hid_set, 16 * f + k + 1)
                mm(Y[:, :], vals_sb[:, k, :], hidden[k % 2][:, :],
                   start=(k == 0), stop=(k == BLOCKS - 1)).then_inc(pe_y, 1)

            def turn(a, t, f, g):
                def fill(part_, step):
                    tile = g if part_ == "joint" else f
                    if tile is not None:
                        for k in blocks_at(part_, step):
                            to_experts(tile, k)

                fill("joint", "begin")
                if t is not None:
                    pe.wait_ge(wide_set, t + 1)
                    for c in range(PAIRS):
                        last = tr(A[1][:, c * P:(c + 1) * P], inv_wide[:, c, :, :], ident)
                    last.then_inc(pe_inv, 1)
                fill("joint", "inverse")
                if t is not None:
                    pe.wait_ge(attnT_set, t + 1)
                    pe.wait_ge(raw_set, 4 * t + 4)
                    for c in range(PAIRS):
                        last = mm(A[0][:, c * P:(c + 1) * P], attnT[:, c * P:(c + 1) * P], woT,
                                  start=True, stop=True)
                    last.then_inc(pe_o, 1)
                fill("joint", "project")
                if f is not None:
                    pe.wait_ge(sq_set, f + 1)
                    mm(R[1][:, :], head_mean, ret_sq[:, :], start=True, stop=True).then_inc(pe_var, 1)
                fill("joint", "variance")
                if a is not None:
                    pe.wait_ge(x_in, 16 * a + 16)
                    after(pe, h_set[0], a)
                    turned(A[0], x_tok).then_inc(pe_xT, 1)
                if g is not None:
                    from_experts(g, BLOCKS - 1)
                if t is not None:
                    pe.wait_ge(c_in, 16 * t + 16)
                    after(pe, ret_set, 4 * t)
                    turned(R[0], c_tok).then_inc(pe_cT, 1)
                if a is not None:
                    pe.wait_ge(xT_set, a + 1)
                    if f is not None:
                        pe.wait_ge(gate_set, f + 1)
                    mm(M[:, :], wqT, xT[:, :], start=True, stop=True).then_inc(pe_q, 1)
                    mm(A[0][:, :], wkT, xT[:, :], start=True, stop=True).then_inc(pe_k, 1)
                if t is not None:
                    pe.wait_ge(cT_set, t + 1)
                    mm(R[0][:, :], wk2[:, :], cT[:, :], start=True, stop=True).then_inc(pe_k2, 1)
                if f is not None:
                    pe.wait_ge(gvar_set, f + 1)
                    pe.wait_ge(gated_set, f + 1)
                    for c in range(PAIRS):
                        last = mm(R[1][:, c * P:(c + 1) * P], gated[:, c * P:(c + 1) * P], wouT,
                                  start=True, stop=True)
                    last.then_inc(pe_out, 1)
                if t is not None:
                    pe.wait_ge(x1_set, 4 * t + 4)
                    turned(A[1], x1_tok).then_inc(pe_x1T, 1)
                if g is not None:
                    pe.wait_ge(yT_set, g + 2)
                    for c in range(PAIRS):
                        last = tr(HB[0][:, c * P:(c + 1) * P], yT[:, c * P:(c + 1) * P], ident)
                    last.then_inc(pe_ytok, 1)
                if a is not None:
                    pe.wait_ge(kT_set, a + 1)
                    token_values(xT, wvT, A[0]).then_inc(pe_v, 1)
                if t is not None:
                    if f is not None:
                        pe.wait_ge(h_set[1], f + 1)
                    mm(R[1][:, :], wk2r[:, :], cT[:, :], start=True, stop=True).then_inc(pe_k2, 1)
                if t is not None:
                    pe.wait_ge(x1T_set, t + 1)
                    if g is not None:
                        pe.wait_ge(h_set[2], g + 2)
                    mm(HB[0][:, :], wq2[:, :], x1T[:, :], start=True, stop=True)
                    mm(Y[:, :], wq2r[:, :], x1T[:, :], start=True, stop=True).then_inc(pe_q2, 1)
                if f is not None:
                    pe.wait_ge(x2_set, 4 * f + 4)
                    turned(HB[1], x2_tok).then_inc(pe_x2T, 1)
                if a is not None:
                    pe.wait_ge(v_set, 4 * a + 4)
                    pe.wait_ge(k_exp_set, 4 * a + 1)
                if f is not None:
                    pe.wait_ge(x2T_set, f + 1)
                    for c in range(PAIRS):
                        last = mm(HB[1][:, c * E:(c + 1) * E], x2T[:, c * P:(c + 1) * P], selT[:, 0:E],
                                  start=True, stop=True)
                    last.then_inc(pe_sel, 1)
                if t is not None:
                    pe.wait_ge(k2_mul, 2 * t + 1)
                    token_values(cT, wv2c[:, :], R[0]).then_inc(pe_v2, 1)

                for p in range(PAIRS):
                    if a is not None:
                        if p == 0:
                            wait_apart(pe, w_rot, 4, qT_set, a + 1)
                        else:
                            wait_apart(pe, w_rot, 4, raw_set, 4 * a + p)
                        for b in range(2):
                            for half in range(2):
                                rows = slice(64 * half, 64 * half + 64)
                                last = mm(A[half][b * S:(b + 1) * S, :], qT[rows, (2 * p + b) * S:(2 * p + b + 1) * S],
                                          k_exp[rows, p % 2, :, b * S:(b + 1) * S], start=True, stop=True)
                        last.then_inc(pe_scores, 1)
                    if t is not None and p == 0:
                        if a is not None:
                            pe.wait_ge(qT_set, a + 1)
                        mm(M[:, :], wgT, x1T[:, :], start=True, stop=True).then_inc(pe_gate, 1)
                        pe.wait_ge(q2_exp_set, 4 * t + 1)
                        pe.wait_ge(v2_set, 2 * t + 2)
                        pe.wait_ge(k2_set, t + 1)
                    if f is not None and p == 0:
                        pe.wait_ge(gates_set, f + 1)
                        tr(HB[1][:, 0:P], gates[:, :, :], ident).then_inc(pe_gates, 1)
                    fill(f"pair{p}", "scores")
                    if t is not None:
                        if p > 0:
                            wait_apart(pe, w_rot, 4, ret_set, 4 * t + p)
                        for b in range(2):
                            for half in range(2):
                                rows = slice(64 * half, 64 * half + 64)
                                last = mm(R[half][b * S:(b + 1) * S, :], k2T[rows, (2 * p + b) * S:(2 * p + b + 1) * S],
                                          q2_exp[rows, p % 2, :, b * S:(b + 1) * S], start=True, stop=True)
                        last.then_inc(pe_sim, 1)
                    if f is not None and p == 0:
                        hidden_of(f, 0)
                    fill(f"pair{p}", "sims")
                    if a is not None:
                        for half in range(2):
                            pe.wait_ge(exp_set, 8 * a + 2 * p + half + 1)
                            for n in range(4):
                                last = tr(A[half][:, n * P:(n + 1) * P], probs[half][:, n * P:(n + 1) * P], ident)
                            last.then_inc(pe_probsT, 1)
                    if t is not None:
                        pe.wait_ge(decayed, 8 * t + 2 * p + 2)
                        retained_values(p, R[0]).then_inc(pe_ret, 1)
                    fill(f"pair{p}", "ret")
                    if t is not None and p + 1 < PAIRS:
                        pe.wait_ge(q2_exp_set, 4 * t + p + 2)
                    if a is not None:
                        pe.wait_ge(probsT_set, 8 * a + 2 * p + 2)
                        if p + 1 < PAIRS:
                            pe.wait_ge(k_exp_set, 4 * a + p + 2)
                        weighted_values(p, lambda b, hp: probsT[hp // 4][
                            :, (hp % 4) * P + b * S:(hp % 4) * P + (b + 1) * S], A[0]).then_inc(pe_attn, 1)
                    fill(f"pair{p}", "weighted")

            pe.wait_ge(w_copied, 2)
            pe.wait_ge(w_rot, 4)
            pe.wait_ge(w_mean, 3)
            pe.wait_ge(w2_in, 16 * 3)
            pe.wait_ge(experts_in, 16 * 2)
            over_tiles(pe, turn)

        @block.scalar
        def _(act):
            run = nc.scalar.activation
            act.preload_act_table_set("natural_log_exp_and_others")
            for n in range(2):
                w = (4, 3)[n]
                act.wait_ge(w_turned, (4, 7)[n])
                run(wT[:, 4 * n:4 * n + w, :], A[n][:, 0:w * P], ACT.Copy).then_inc(w_copied, 1)
            act.wait_ge(bias_in, 32)
            run(gb_neg[:, :], gb[:, :], ACT.Copy, scale=-1.0).then_inc(w_copied, 1)
            act.wait_ge(w_copied, 3)
            act.sem_inc(yT_set, 1)
            act.wait_ge(pads_set, 2)

            def values_out():
                for h2 in range(2):
                    d = slice(HD * h2, HD * h2 + HD)
                    for b in range(2):
                        own = A[0][S * b:S * b + S, :].rearrange("p (n e d) -> p n e d", e=2, d=16)
                        run(v_pad[64 * h2:64 * h2 + 64, b, :, 0:4:3, d], own[:, :, :, d], ACT.Copy).then_inc(v_set, 1)

            def root(n, i):
                act.wait_ge(mo_set[n], 4 * i + 4)
                run(var_ln[n][:, :], moments[n][:, :, 1:2].rearrange("p c o -> p (c o)"), ACT.Ln,
                    bias=eps).then_inc(ln_set[n], 1)
                act.wait_ge(ln_set[n], i + 1)
                run(rstd[n][:, :], var_ln[n][:, :], ACT.Exp, scale=-0.5).then_inc(rs_set[n], 1)

            def turn(a, t, f, g):
                if f is not None:
                    act.wait_ge(ret_set, 4 * f + 4)
                    run(ret_sq[:, :], ret_sep[:, :], ACT.Square).then_inc(sq_set, 1)
                if t is not None:
                    root(0, t)
                if f is not None:
                    act.wait_ge(pe_var, f + 1)
                    run(gvar[:, :], R[1][:, :], ACT.Ln, bias=eps).then_inc(gvar_set, 1)
                    act.wait_ge(gvar_set, f + 1)
                    run(grs[:, :], gvar[:, :], ACT.Exp, scale=-0.5).then_inc(grs_set, 1)
                if a is not None:
                    act.wait_ge(pe_xT, a + 1)
                    run(xT[:, :], A[0][:, :], ACT.Copy).then_inc(xT_set, 1)
                if t is not None:
                    act.wait_ge(pe_cT, t + 1)
                    run(cT[:, :], R[0][:, :], ACT.Copy).then_inc(cT_set, 1)
                if g is not None:
                    act.wait_ge(pe_y, 16 * g + 16)
                    run(yT[:, :], Y[:, :], ACT.Copy).then_inc(yT_set, 1)
                if a is not None:
                    act.wait_ge(pe_k, a + 1)
                    run(kT[:, :], A[0][:, :], ACT.Copy).then_inc(kT_set, 1)
                    act.wait_ge(pe_q, a + 1)
                    run(qT[:, :], M[:, :], ACT.Copy).then_inc(qT_set, 1)
                if t is not None:
                    act.wait_ge(pe_x1T, t + 1)
                    run(x1T[:, :], A[1][:, :], ACT.Copy).then_inc(x1T_set, 1)
                if a is not None:
                    act.wait_ge(pe_v, a + 1)
                    values_out()
                if f is not None:
                    root(1, f)
                if f is not None:
                    act.wait_ge(pe_x2T, f + 1)
                    run(x2T[:, :], HB[1][:, :], ACT.Copy).then_inc(x2T_set, 1)
                    act.wait_ge(pe_sel, f + 1)
                    run(sel_e[:, :, :], HB[1][:, 0:PAIRS * E], ACT.Exp, scale=-1.0).then_inc(sel_exp, 1)
                if t is not None:
                    act.wait_ge(pe_v2, t + 1)
                    for b in range(2):
                        rows = slice(S * b, S * b + S)
                        own = v2_pad[rows, :, :, :].rearrange("p c n (h w) -> p (c n) h w", w=72)
                        run(own[:, :, :, 32 * b:32 * b + HD],
                            R[0][rows, :].rearrange("p (m h d) -> p m h d", h=4, d=HD), ACT.Copy).then_inc(v2_set, 1)
                if a is not None:
                    act.wait_ge(x_in, 16 * a + 16)
                    after(act, h_set[0], a)
                    run(xr_tok[:, :, :], x_tok[:, :, :], ACT.Copy).then_inc(xr_set, 1)
                if t is not None:
                    act.wait_ge(pe_gate, t + 1)
                    run(sw_e[:, :], M[:, :], ACT.Exp, scale=-1.0, bias=gb_neg[:, :]).then_inc(sw_exp, 1)
                if f is not None:
                    act.wait_ge(pe_gates, f + 1)
                    after(act, gates_out, 16 * f)
                    run(gatesT[:, :], HB[1][:, 0:P], ACT.Copy).then_inc(gatesT_set, 1)
                for p in range(PAIRS):
                    if a is not None:
                        for half in range(2):
                            act.wait_ge(shifted, 8 * a + 2 * p + half + 1)
                            run(probs[half][:, :], probs[half][:, :], ACT.Exp, scale=SCALE).then_inc(exp_set, 1)
                    if a is not None:
                        for half in range(2):
                            act.wait_ge(pe_probsT, 8 * a + 2 * p + half + 1)
                            run(probsT[half][:, :], A[half][:, :], ACT.Copy).then_inc(probsT_set, 1)
                    if t is not None and p == 0:
                        act.wait_ge(sw_exp, t + 1)
                        run(sw_l[:, :], sw_e[:, :], ACT.Ln, bias=one).then_inc(sw_log, 1)
                        act.wait_ge(sw_log, t + 1)
                        run(sw_r[:, :], sw_l[:, :], ACT.Exp, scale=-1.0).then_inc(sw_inv, 1)
                    if t is not None:
                        act.wait_ge(pe_ret, 4 * t + p + 1)
                        run(ret_sep[:, p * P:(p + 1) * P], R[0][:, 0:P], ACT.Copy).then_inc(ret_set, 1)
                    if a is not None:
                        act.wait_ge(pe_attn, 4 * a + p + 1)
                        run(rawT[:, p * P:(p + 1) * P], A[0][:, 0:P], ACT.Copy).then_inc(raw_set, 1)
                    if g is not None and p == 0:
                        root(2, g)

            over_tiles(act, turn)

        @block.vector
        def _(dve):
            v = nc.vector
            v.memset(raw_w[:, 6, :], 0.0).then_inc(raw_zero, 1)
            v.memset(sel_g[:, :, E:E + MAX8 - TOP], -1.0).then_inc(zeros_set, 1)
            v.memset(tops[:, :, :], -1.0).then_inc(zeros_set, 1)
            dve.wait_ge(zeros_set, 2)
            dve.wait_ge(w2_in, 16 * 3)
            for w, wr in ((wq2, wq2r), (wk2, wk2r)):
                even_odd = w[:, :].rearrange("p (n two) -> p n two", two=2)
                rotated = wr[:, :].rearrange("p (n two) -> p n two", two=2)
                v.tensor_scalar(rotated[:, :, 0:1], even_odd[:, :, 1:2], -1.0, None, ALU.mult).then_inc(w_rot, 1)
                v.tensor_copy(rotated[:, :, 1:2], even_odd[:, :, 0:1]).then_inc(w_rot, 1)
            heads = wv2[:, :].rearrange("p (h e) -> p h e", e=HD)
            v.tensor_reduce(head_sum[:, 0, :], heads, axis=AX.X, op=ALU.add).then_inc(w_mean, 1)
            dve.wait_ge(w_mean, 1)
            v.tensor_scalar(head_sum[:, 1, :], head_sum[:, 0, :], 1.0 / HD, None, ALU.mult).then_inc(w_mean, 1)
            dve.wait_ge(w_mean, 2)
            v.tensor_tensor(wv2c[:, :].rearrange("p (h e) -> p h e", e=HD), heads,
                            head_sum[:, 1, :].rearrange("p (h o) -> p h o", o=1).broadcast_to([P, H, HD]),
                            ALU.subtract).then_inc(w_mean, 1)
            dve.wait_ge(consts_in, 16)
            dve.wait_ge(bias_in, 32)
            dve.sem_inc(h_set[2], 1)

            def norm_stats(n, i):
                for c in range(PAIRS):
                    v.bn_stats(stats[n][:, c, :], h_tok[n][:, c, :]).then_inc(st_set[n], 1)
                dve.wait_ge(st_set[n], 4 * i + 4)
                v.memset(spare[:, :], 0.0)
                for c in range(PAIRS):
                    v.bn_aggr(moments[n][:, c, :], stats[n][:, c, :]).then_inc(mo_set[n], 1)

            def norm_apply(n, i, dst, done):
                dve.wait_ge(mo_set[n], 4 * i + 4)
                dve.wait_ge(rs_set[n], i + 1)
                for c in range(PAIRS):
                    v.tensor_scalar(dst[:, c, :], h_tok[n][:, c, :], moments[n][:, c, 0:1], rstd[n][:, c:c + 1],
                                    ALU.subtract, ALU.mult).then_inc(done, 1)

            def gate_block(f, k):
                if k in GATE_PARTS:
                    dve.wait_ge(gates_in[GATE_PARTS.index(k)], 32 * f + 32)
                dve.wait_ge(pe_hid, 16 * f + k + 1)
                if k >= 2:
                    dve.wait_ge(pe_y, 16 * f + k - 1)
                v.scalar_tensor_tensor(out=hidden[k % 2][:, :], in0=HB[k % 2][:, :], scalar=0.0,
                                       in1=gate_bc[:, k, :], op0=ALU.max, op1=ALU.mult).then_inc(hid_set, 1)

            def over_seqs(ap):
                return ap.rearrange("p (a t) -> p a t", a=1).broadcast_to([P, SEQS, S])

            def seqs(ap):
                return ap.rearrange("p (a t) -> p a t", t=S)

            def toks(bank):
                return bank[:, :].rearrange("p (c d) -> p c d", c=PAIRS)

            def turn(a, t, f, g):
                def fill(part_, step):
                    tile = g if part_ == "joint" else f
                    if tile is not None:
                        for k in blocks_at(part_, step):
                            gate_block(tile, k)

                fill("joint", "begin")
                if t is not None:
                    dve.wait_ge(raw_set, 4 * t + 4)
                    dve.wait_ge(pe_inv, t + 1)
                    v.tensor_tensor(attnT[:, :], A[1][:, :], rawT[:, :], ALU.mult).then_inc(attnT_set, 1)
                fill("joint", "inverse")
                if t is not None:
                    dve.wait_ge(pe_o, t + 1)
                    dve.wait_ge(xr_set, t + 1)
                    v.tensor_tensor(h_tok[0][:, :, :], toks(A[0]), xr_tok[:, :, :], ALU.add).then_inc(h_set[0], 1)
                    dve.wait_ge(h_set[0], t + 1)
                    norm_stats(0, t)
                fill("joint", "project")
                fill("joint", "variance")
                if t is not None:
                    if f is not None:
                        dve.wait_ge(x1b_set, f + 1)
                        dve.wait_ge(pe_gate, f + 1)
                    norm_apply(0, t, x1_tok, x1_set)
                if f is not None:
                    dve.wait_ge(grs_set, f + 1)
                    dve.wait_ge(gate_set, f + 1)
                    for half in range(2):
                        for b in range(2):
                            for q in range(2):
                                rows, n = slice(64 * half + 32 * b, 64 * half + 32 * b + 32), 2 * half + q
                                v.tensor_tensor(
                                    retT[32 * n:32 * n + 32, :].rearrange("p (c b s) -> p c b s", b=2, s=S)[:, :, b, :],
                                    ret_sep[rows, :].rearrange("p (c q s) -> p c q s", q=2, s=S)[:, :, q, :],
                                    grs[rows, :].rearrange("p (c q s) -> p c q s", q=2, s=S)[:, :, q, :],
                                    ALU.mult).then_inc(retT_set, 1)
                    dve.wait_ge(retT_set, 8 * f + 8)
                    v.tensor_tensor(gated[:, :], retT[:, :], gateT[:, :], ALU.mult).then_inc(gated_set, 1)
                if t is not None:
                    dve.wait_ge(pe_k2, 2 * t + 1)
                    after(dve, k2_set, t)
                    v.tensor_tensor(seqs(k2c[:, :]), seqs(R[0][:, :]), over_seqs(k_cos), ALU.mult).then_inc(k2_mul, 1)
                if f is not None:
                    dve.wait_ge(pe_out, f + 1)
                    dve.wait_ge(x1b_set, f + 1)
                    v.tensor_tensor(h_tok[1][:, :, :], toks(R[1]), x1b_tok[:, :, :], ALU.add).then_inc(h_set[1], 1)
                    dve.wait_ge(h_set[1], f + 1)
                    norm_stats(1, f)
                if g is not None:
                    dve.wait_ge(pe_ytok, g + 1)
                    dve.wait_ge(x2c_set, g + 1)
                    v.tensor_tensor(h_tok[2][:, :, :], toks(HB[0]), x2c_tok[:, :, :], ALU.add).then_inc(h_set[2], 1)
                if f is not None:
                    norm_apply(1, f, x2_tok, x2_set)
                if t is not None:
                    dve.wait_ge(pe_k2, 2 * t + 2)
                    v.tensor_tensor(seqs(k2s[:, :]), seqs(R[1][:, :]), over_seqs(k_sin), ALU.mult).then_inc(k2_mul, 1)
                    dve.wait_ge(pe_q2, t + 1)
                    v.tensor_tensor(seqs(q2c[:, :]), seqs(HB[0][:, :]), over_seqs(q_cos), ALU.mult).then_inc(q2_mul, 1)
                    v.tensor_tensor(seqs(q2s[:, :]), seqs(Y[:, :]), over_seqs(q_sin), ALU.mult).then_inc(q2_mul, 1)
                if f is not None:
                    dve.wait_ge(sel_exp, f + 1)
                    v.tensor_scalar(sel_d[:, :, :], sel_e[:, :, :], 1.0, None, ALU.add).then_inc(sel_add, 1)
                    dve.wait_ge(sel_add, f + 1)
                    v.reciprocal(sel_g[:, :, 0:E], sel_d[:, :, :]).then_inc(sel_inv, 1)
                    wait_apart(dve, zeros_set, 2, sel_inv, f + 1)
                    for c in range(PAIRS):
                        v.max(tops[:, c, :], sel_g[:, c, 0:E]).then_inc(top_set, 1)
                    dve.wait_ge(top_set, 4 * f + 4)
                    v.memset(tops[:, :, TOP:MAX8], -1.0).then_inc(top_cut, 1)
                    wait_apart(dve, zeros_set, 2, top_cut, f + 1)
                    for c in range(PAIRS):
                        v.match_replace(out=sel_m[:, c, :], in_to_replace=tops[:, c, :],
                                        in_values=sel_g[:, c, :], imm_value=0.0).then_inc(matched, 1)
                    dve.wait_ge(matched, 4 * f + 4)
                    v.tensor_tensor(gates[:, :, :], sel_g[:, :, 0:E], sel_m[:, :, 0:E],
                                    ALU.subtract).then_inc(gates_set, 1)

                for p in range(PAIRS):
                    if a is not None:
                        dve.wait_ge(pe_scores, 4 * a + p + 1)
                        for half in range(2):
                            n = 8 * a + 2 * p + half
                            after(dve, sum_set, n - 1)
                            v.tensor_tensor(seqs(probs[half][:, :]), seqs(A[half][:, :]), over_seqs(causal),
                                            ALU.add).then_inc(masked, 1)
                            dve.wait_ge(masked, n + 1)
                            v.tensor_reduce(row_max[:, half, :], seqs(probs[half][:, :]), axis=AX.X,
                                            op=ALU.max).then_inc(max_set, 1)
                    fill(f"pair{p}", "scores")
                    if t is not None:
                        dve.wait_ge(pe_sim, 4 * t + p + 1)
                        for half in range(2):
                            v.tensor_tensor(simT[half][:, :], R[half][:, :], decay[:, 8 * half * S:8 * (half + 1) * S],
                                            ALU.mult).then_inc(decayed, 1)
                    if g is not None and p == 0:
                        dve.wait_ge(h_set[2], g + 2)
                        norm_stats(2, g)
                    fill(f"pair{p}", "sims")
                    if a is not None:
                        for half in range(2):
                            dve.wait_ge(exp_set, 8 * a + 2 * p + half + 1)
                            v.tensor_reduce(row_sum[:, p, half, :], seqs(probs[half][:, :]), axis=AX.X,
                                            op=ALU.add).then_inc(sum_set, 1)
                    if t is not None and p == 0:
                        dve.wait_ge(sw_inv, t + 1)
                        v.scalar_tensor_tensor(out=gateT[:, :], in0=M[:, :], scalar=gb[:, :], in1=sw_r[:, :],
                                               op0=ALU.add, op1=ALU.mult).then_inc(gate_set, 1)
                    fill(f"pair{p}", "ret")
                    if a is not None and p == PAIRS - 1:
                        dve.wait_ge(sum_set, 8 * a + 8)
                        v.reciprocal(row_inv[:, :, :],
                                     row_sum[:, :, :, :].rearrange("p c g j -> p c (g j)")).then_inc(inv_set, 1)
                    fill(f"pair{p}", "weighted")
                    if g is not None and p == 0:
                        dve.wait_ge(stored, 16 * g + 16)
                        norm_apply(2, g, out_tok, out_set)

            over_tiles(dve, turn)

        @block.gpsimd
        def _(pool):
            gp = nc.gpsimd
            gp.memset(v_pad[:, :, :, :, :], 0.0).then_inc(pads_set, 1)
            gp.memset(v2_pad[:, :, :, :], 0.0).then_inc(pads_set, 1)
            pool.wait_ge(consts_in, 16)
            pool.wait_ge(bias_in, 32)

            def expand(src, p, dst, done):
                heads = src[:, p * P:(p + 1) * P].rearrange("p (a t) -> p a t", a=1).broadcast_to([P, 8, P])
                pick = head_pick.rearrange("p (a t) -> p a t", t=1).broadcast_to([P, 8, P])
                gp.tensor_tensor(dst[:, p % 2, :, :], heads, pick, ALU.mult).then_inc(done, 1)

            def turn(a, t, f, g):
                if a is not None:
                    pool.wait_ge(kT_set, a + 1)
                    expand(kT, 0, k_exp, k_exp_set)
                    expand(kT, 1, k_exp, k_exp_set)
                if t is not None:
                    pool.wait_ge(k2_mul, 2 * t + 2)
                    gp.tensor_tensor(k2T[:, :], k2c[:, :], k2s[:, :], ALU.add).then_inc(k2_set, 1)
                    pool.wait_ge(q2_mul, 2 * t + 2)
                    gp.tensor_tensor(q2T[:, :], q2c[:, :], q2s[:, :], ALU.add).then_inc(q2_set, 1)
                    pool.wait_ge(q2_set, t + 1)
                    expand(q2T, 0, q2_exp, q2_exp_set)
                for p in range(PAIRS):
                    if a is not None:
                        for half in range(2):
                            pool.wait_ge(max_set, 8 * a + 2 * p + half + 1)
                            top = row_max[:, half, :].rearrange("p (a o) -> p a o", o=1).broadcast_to([P, 8, S])
                            s = probs[half][:, :].rearrange("p (a t) -> p a t", t=S)
                            gp.tensor_tensor(s, s, top, ALU.subtract).then_inc(shifted, 1)
                    if t is not None and p == 0:
                        expand(q2T, 1, q2_exp, q2_exp_set)
                    if t is not None and p + 2 < PAIRS:
                        pool.wait_ge(pe_sim, 4 * t + p + 1)
                        expand(q2T, p + 2, q2_exp, q2_exp_set)
                    if a is not None and p + 2 < PAIRS:
                        expand(kT, p + 2, k_exp, k_exp_set)
                    if t is not None and p == 1:
                        pool.wait_ge(x1_set, 4 * t + 4)
                        if f is not None:
                            pool.wait_ge(x2_set, 4 * f + 4)
                        gp.tensor_tensor(x1b_tok[:, :, :], x1_tok[:, :, :],
                                         ob[:, :].rearrange("p (a d) -> p a d", a=1).broadcast_to([P, PAIRS, D]),
                                         ALU.add).then_inc(x1b_set, 1)
                    if f is not None and p == 1:
                        if t is None:
                            pool.wait_ge(x2_set, 4 * f + 4)
                        gp.tensor_copy(x2c_tok[:, :, :], x2_tok[:, :, :]).then_inc(x2c_set, 1)
                if a is not None:
                    wait_apart(pool, bias_in, 32, inv_set, a + 1)
                    wide = row_inv[:, :, :].rearrange("p c h -> p (c h)").rearrange("p (a o) -> p a o", o=1)
                    gp.tensor_copy(inv_wide[:, :, :, :].rearrange("p c h d -> p (c h) d"),
                                   wide.broadcast_to([P, PAIRS * H, HD])).then_inc(wide_set, 1)

            over_tiles(pool, turn)


def constant_table():
    import numpy as np
    P, S, H, HD = 128, 64, 16, 8
    p = np.arange(P)
    same_head = (p[:, None] // HD == p[None, :] // HD) / HD
    causal = np.where(np.arange(S)[None, :] <= (p % S)[:, None], 0.0, -3.0e38)
    f4 = np.float32
    gammas = (1.0 - np.exp(np.linspace(np.log(1.0 / 32.0), np.log(1.0 / 512.0), H).astype(f4))).astype(f4)
    dist = np.arange(S)[None, None, :] - (p % S)[:, None, None]
    decay = np.where(dist >= 0, gammas[None, :, None].astype(np.float64) ** np.maximum(dist, 0), 0.0)
    base = ((np.arange(0, HD, 2) + 0.4 * HD) / (1.4 * HD)).astype(f4).astype(np.float64)
    power = np.arange(-(S // 2), S - S // 2) / 512.0
    scale = base[None, :] ** power[:, None]
    inv_freq = (1.0 / 10000.0 ** (np.arange(HD // 2, dtype=f4) / f4(HD // 2))).astype(f4)
    ang = (np.arange(S, dtype=f4)[:, None] * inv_freq[None, :]).astype(np.float64)
    rows = (p % HD) // 2
    turns = [t[:, rows].T for t in (np.cos(ang) * scale, np.sin(ang) * scale,
                                    np.cos(ang) / scale, np.sin(ang) / scale)]
    pick = ((p // HD) % 8)[:, None] == np.arange(8)[None, :]
    return np.ascontiguousarray(np.concatenate(
        [np.eye(P), same_head, causal, decay.reshape(P, -1), *turns, pick,
         np.full((P, 1), 1e-5), np.ones((P, 1))], axis=1).astype(f4))


_INS = ["x", "ctx_1024", "L0_attn_q_proj", "L0_attn_k_proj", "L0_attn_v_proj", "L0_attn_o_proj",
        "L0_xattn_W_Q", "L0_xattn_W_K", "L0_xattn_W_V", "L0_xattn_g_w", "L0_xattn_g_b",
        "L0_xattn_out_w", "L0_xattn_out_b", "L0_ffn_expert_sel", "L0_ffn_keys", "L0_ffn_values"]


def kernel(**inputs):
    import numpy as np
    import concourse.bacc as bacc
    from concourse import mybir
    from concourse.bass_utils import run_bass_kernel_spmd as run

    nc = bacc.Bacc("TRN2", target_bir_lowering=False, num_devices=1)
    arrays, args = {}, []
    named = [(name, np.ascontiguousarray(inputs[name])) for name in _INS] + [("consts", constant_table())]
    for name, a in named:
        arrays[f"in_{name}"] = a
        args.append(nc.dram_tensor(f"in_{name}", a.shape, mybir.dt.from_np(a.dtype), kind="ExternalInput").ap())
    args.append(nc.dram_tensor("out_0", inputs["x"].shape, mybir.dt.float32, kind="ExternalOutput").ap())
    decoder_layer(nc, *args)
    r = run(nc, [arrays], core_ids=[0])
    return r.results[0]["out_0"]
```

```python
import concourse.bass as bass
from concourse import mybir
from contextlib import ExitStack


def decoder_layer(nc: bass.Bass, x, ctx_in, q_proj, k_proj, v_proj, o_proj, W_Q, W_K, W_V, g_w, g_b,
                  out_w, out_b, expert_sel, keys, values, consts, out):
    f32, f32r = mybir.dt.float32, mybir.dt.float32r
    ALU = mybir.AluOpType
    ACT = mybir.ActivationFunctionType
    AX = mybir.AxisListType

    BATCH, S, D = x.shape
    H, _, HD = W_Q.shape
    E, _, F = keys.shape
    P = 128
    TOK = 512
    TILES = BATCH * S // TOK
    PAIRS = TOK // P
    SEQS = TOK // S
    QUADS = 4
    BLOCKS = E * F // P
    TOP = 4
    HALVES = (1, 0)
    GATE_PARTS = (0, 2, 4, 8)
    MAX8 = 8
    SCALE = float(HD) ** -0.5

    x_tiles = x.rearrange("b s d -> (b s) d").rearrange("(t c p) d -> t p c d", c=PAIRS, p=P)
    ctx_tiles = ctx_in.rearrange("b s d -> (b s) d").rearrange("(t c p) d -> t p c d", c=PAIRS, p=P)
    out_tiles = out.rearrange("b s d -> (b s) d").rearrange("(t c p) d -> t p c d", c=PAIRS, p=P)
    gate_rows = nc.dram_tensor("gate_rows", (E, TOK), f32, kind="Internal").ap()

    stack = ExitStack()
    with stack:
        def sb(name, shape, dtype=f32):
            return stack.enter_context(nc.sbuf_tensor(name, shape, dtype))

        def ps(name):
            return stack.enter_context(nc.psum_tensor(name, [P, 512], f32))

        def sem(name):
            return stack.enter_context(nc.semaphore(name))

        const = sb("const", [P, consts.shape[1]])
        col = [0]

        def part(n):
            col[0] += n
            return const[:, col[0] - n:col[0]]

        ident = part(P)
        head_mean = part(P)
        causal = part(S)
        decay = part(H * S)
        q_cos, q_sin, k_cos, k_sin = part(S), part(S), part(S), part(S)
        head_pick = part(8)
        eps = part(1)
        one = part(1)

        raw_w = sb("raw_w", [P, 7, P])
        wT = sb("wT", [P, 7, P])
        wqT, wkT, wvT, woT, wgT, wouT, selT = (wT[:, n, :] for n in range(7))
        wq2, wk2, wv2 = sb("wq2", [P, P]), sb("wk2", [P, P]), sb("wv2", [P, P])
        wq2r, wk2r = sb("wq2r", [P, P]), sb("wk2r", [P, P])
        wv2c = sb("wv2c", [P, P])
        head_sum = sb("head_sum", [P, 2, H])
        keys_hi, keys_lo = sb("keys_hi", [P, E * F], f32r), sb("keys_lo", [P, E * F], f32r)
        vals_sb = sb("vals_sb", [P, BLOCKS, P])
        gb, gb_neg = sb("gb", [P, 1]), sb("gb_neg", [P, 1])
        ob = sb("ob", [P, P])

        x_tok, xT = sb("x_tok", [P, PAIRS, D]), sb("xT", [P, TOK])
        xr_tok = sb("xr_tok", [P, PAIRS, D])
        qT, kT = sb("qT", [P, TOK]), sb("kT", [P, TOK])
        k_exp = sb("k_exp", [P, 2, 8, P])
        v_pad = sb("v_pad", [P, 2, PAIRS * QUADS, 4, 16])
        probs = [sb(f"probs{g}", [P, 512]) for g in range(2)]
        probsT = [sb(f"probsT{g}", [P, 512]) for g in range(2)]
        row_max = sb("row_max", [P, 2, 8])
        row_sum = sb("row_sum", [P, PAIRS, 2, 8])
        row_inv = sb("row_inv", [P, PAIRS, H])
        inv_wide = sb("inv_wide", [P, PAIRS, H, HD])
        rawT, attnT = sb("rawT", [P, TOK]), sb("attnT", [P, TOK])
        x1_tok, x1T = sb("x1_tok", [P, PAIRS, D]), sb("x1T", [P, TOK])
        c_tok, cT = sb("c_tok", [P, PAIRS, D]), sb("cT", [P, TOK])
        x1b_tok = sb("x1b_tok", [P, PAIRS, D])
        k2c, k2s, q2c, q2s = sb("k2c", [P, TOK]), sb("k2s", [P, TOK]), sb("q2c", [P, TOK]), sb("q2s", [P, TOK])
        k2T, q2T = sb("k2T", [P, TOK]), sb("q2T", [P, TOK])
        q2_exp = sb("q2_exp", [P, 2, 8, P])
        v2_pad = sb("v2_pad", [P, PAIRS, QUADS, 4 * 72])
        simT = [sb(f"simT{g}", [P, 512]) for g in range(2)]
        sw, gateT = sb("sw", [P, TOK]), sb("gateT", [P, TOK])
        ret_sep, ret_sq = sb("ret_sep", [P, TOK]), sb("ret_sq", [P, TOK])
        grs, gated = sb("grs", [P, TOK]), sb("gated", [P, TOK])
        x2_tok, x2T = sb("x2_tok", [P, PAIRS, D]), sb("x2T", [P, TOK])
        x2T_hi, x2T_lo = sb("x2T_hi", [P, TOK], f32r), sb("x2T_lo", [P, TOK], f32r)
        sel_e, sel_d = sb("sel_e", [P, PAIRS, E]), sb("sel_d", [P, PAIRS, E])
        sel_g = sb("sel_g", [P, PAIRS, E + MAX8 - TOP])
        sel_m = sb("sel_m", [P, PAIRS, E + MAX8 - TOP])
        tops = sb("tops", [P, PAIRS, MAX8])
        gates, gatesT = sb("gates", [P, PAIRS, E]), sb("gatesT", [P, P])
        gate_bc = sb("gate_bc", [P, BLOCKS, TOK])
        x2c_tok = sb("x2c_tok", [P, PAIRS, D])
        hidden = [sb(f"hidden{n}", [P, TOK]) for n in range(2)]
        yT, out_tok = sb("yT", [P, TOK]), sb("out_tok", [P, PAIRS, D])
        h_tok = [sb(f"h{n}_tok", [P, PAIRS, D]) for n in range(3)]
        stats = [sb(f"stats{n}", [P, PAIRS, 6]) for n in range(3)]
        moments = [sb(f"moments{n}", [P, PAIRS, 2]) for n in range(3)]
        var_ln = [sb(f"var_ln{n}", [P, PAIRS]) for n in range(3)]
        rstd = [sb(f"rstd{n}", [P, PAIRS]) for n in range(3)]
        spare = sb("spare", [P, 1])

        A = [ps("attn0"), ps("attn1")]
        R = [ps("ret0"), ps("ret1")]
        M = ps("third")
        HB = [ps("hid0"), ps("hid1")]
        Y = ps("expert_sum")

        consts_in, raw_in, w2_in, experts_in, bias_in = (sem(n) for n in (
            "consts_in", "raw_in", "w2_in", "experts_in", "bias_in"))
        zeros_set, raw_zero, pads_set = sem("zeros_set"), sem("raw_zero"), sem("pads_set")
        w_turned, w_copied, w_rot, w_mean = sem("w_turned"), sem("w_copied"), sem("w_rot"), sem("w_mean")
        xr_set = sem("xr_set")
        x_in, c_in = sem("x_in"), sem("c_in")
        pe_xT, pe_k, pe_q, xT_set, kT_set, qT_set = (sem(n) for n in (
            "pe_xT", "pe_k", "pe_q", "xT_set", "kT_set", "qT_set"))
        pe_v, v_set, k_exp_set = sem("pe_v"), sem("v_set"), sem("k_exp_set")
        pe_scores = sem("pe_scores")
        masked, max_set, shifted, exp_set, sum_set, pe_probsT, probsT_set = (sem(n) for n in (
            "masked", "max_set", "shifted", "exp_set", "sum_set", "pe_probsT", "probsT_set"))
        pe_attn, raw_set = sem("pe_attn"), sem("raw_set")
        inv_set, wide_set, pe_inv, attnT_set, pe_o, pe_x1T, x1T_set = (sem(n) for n in (
            "inv_set", "wide_set", "pe_inv", "attnT_set", "pe_o", "pe_x1T", "x1T_set"))
        pe_cT, cT_set, x1b_set, pe_k2, k2_set, pe_q2, q2_set = (sem(n) for n in (
            "pe_cT", "cT_set", "x1b_set", "pe_k2", "k2_set", "pe_q2", "q2_set"))
        k2_mul, q2_mul, q2_exp_set, pe_v2, v2_set = (sem(n) for n in (
            "k2_mul", "q2_mul", "q2_exp_set", "pe_v2", "v2_set"))
        pe_gate, sw_exp, sw_log, sw_inv, gate_set = (sem(n) for n in (
            "pe_gate", "sw_exp", "sw_log", "sw_inv", "gate_set"))
        pe_sim, decayed, pe_ret, ret_set = (sem(n) for n in (
            "pe_sim", "decayed", "pe_ret", "ret_set"))
        sq_set, pe_var, gvar_set, grs_set, retT_set, gated_set = (sem(n) for n in (
            "sq_set", "pe_var", "gvar_set", "grs_set", "retT_set", "gated_set"))
        pe_out, pe_x2T, x2T_set, pe_sel, sel_exp, sel_add, sel_inv = (sem(n) for n in (
            "pe_out", "pe_x2T", "x2T_set", "pe_sel", "sel_exp", "sel_add", "sel_inv"))
        top_set, top_cut, matched, gates_set, pe_gates, gatesT_set = (sem(n) for n in (
            "top_set", "top_cut", "matched", "gates_set", "pe_gates", "gatesT_set"))
        gates_out = sem("gates_out")
        gates_in = [sem(f"gates_in{n}") for n in range(len(GATE_PARTS))]
        keys_split, x2T_split = sem("keys_split"), sem("x2T_split")
        x2c_set, pe_hid, hid_set, pe_y, yT_set, pe_ytok = (sem(n) for n in (
            "x2c_set", "pe_hid", "hid_set", "pe_y", "yT_set", "pe_ytok"))
        h_set = [sem(f"h{n}_set") for n in range(3)]
        st_set, mo_set = [sem(f"st{n}_set") for n in range(3)], [sem(f"mo{n}_set") for n in range(3)]
        ln_set, rs_set = [sem(f"ln{n}_set") for n in range(3)], [sem(f"rs{n}_set") for n in range(3)]
        x1_set, x2_set, out_set = sem("x1_set"), sem("x2_set"), sem("out_set")
        stored = sem("stored")

        block = stack.enter_context(nc.Block())

        def over_tiles(engine, turn):
            turn(0, None, None, None)
            turn(1, 0, None, None)
            turn(2, 1, 0, None)
            with engine.Fori(3, TILES) as i:
                turn(i, i - 1, i - 2, i - 3)
            turn(None, TILES - 1, TILES - 2, TILES - 3)
            turn(None, None, TILES - 1, TILES - 2)
            turn(None, None, None, TILES - 1)

        def after(engine, semaphore, value):
            if not isinstance(value, int) or value > 0:
                engine.wait_ge(semaphore, value)

        def wait_apart(engine, fixed, count, semaphore, value):
            engine.wait_ge(fixed, count)
            engine.wait_ge(semaphore, value)

        FILL = [("pair0", "scores", 0), ("pair0", "sims", 0), ("pair0", "ret", 0), ("pair0", "weighted", 1),
                ("pair1", "scores", 1), ("pair1", "sims", 1), ("pair1", "ret", 1), ("pair1", "weighted", 0),
                ("pair2", "scores", 1), ("pair2", "sims", 1), ("pair2", "ret", 1), ("pair2", "weighted", 0),
                ("pair3", "scores", 1), ("pair3", "sims", 1), ("pair3", "ret", 1), ("pair3", "weighted", 0),
                ("joint", "begin", 1), ("joint", "inverse", 1), ("joint", "project", 1),
                ("joint", "variance", 1), ("joint", "late", 1), ("joint", "after", 1)]
        assert sum(n for _, _, n in FILL) == BLOCKS

        def blocks_at(part_, step):
            at = 0
            for p_, s_, n in FILL:
                if (p_, s_) == (part_, step):
                    return range(at, at + n)
                at += n

        @block.sync
        def _(sp):
            sp.sem_inc(stored, 16)
            sp.dma_start(const[:, :], consts).then_inc(consts_in, 16)
            sp.dma_start(x_tok[:, :, :], x_tiles[0]).then_inc(x_in, 16)
            for n, w in enumerate((q_proj, k_proj, v_proj, o_proj, g_w, out_w)):
                sp.dma_start(raw_w[:, n, :], w).then_inc(raw_in, 16)
            sp.wait_ge(raw_zero, 1)
            sp.dma_start(raw_w[0:E, 6, :], expert_sel).then_inc(raw_in, 16)
            for dst, w in ((wq2, W_Q), (wk2, W_K), (wv2, W_V)):
                sp.dma_start(dst[:, :].rearrange("d (h e) -> d h e", h=H),
                             w.rearrange("h d e -> d h e")).then_inc(w2_in, 16)
            sp.dma_start(gb[:, :], g_b.rearrange("(d a) -> d a", a=1)).then_inc(bias_in, 16)
            sp.dma_start(ob[:, :], out_b.rearrange("(a d) -> a d", a=1).broadcast_to([P, D])).then_inc(bias_in, 16)
            sp.dma_start(c_tok[:, :, :], ctx_tiles[0]).then_inc(c_in, 16)
            sp.dma_start(gate_bc[:, 0:E * F // TOK, :].rearrange("p b (e f) -> p (b e) f", f=F), keys.rearrange("e d f -> d e f")).then_inc(experts_in, 16)
            sp.dma_start(vals_sb[:, :, :], values.rearrange("e f v -> (e f) v")
                         .rearrange("(b p) v -> p b v", p=P)).then_inc(experts_in, 16)

            def turn(a, t, f, g, more_x=True, more_c=True):
                if t is not None and more_c:
                    sp.wait_ge(pe_cT, t + 1)
                    sp.dma_start(c_tok[:, :, :], ctx_tiles[t + 1]).then_inc(c_in, 16)
                if a is not None and more_x:
                    sp.wait_ge(pe_xT, a + 1)
                    sp.wait_ge(xr_set, a + 1)
                    sp.dma_start(x_tok[:, :, :], x_tiles[a + 1]).then_inc(x_in, 16)
                if f is not None:
                    sp.wait_ge(gatesT_set, f + 1)
                    sp.dma_start(gate_rows.rearrange("e (c p) -> c e p", c=PAIRS),
                                 gatesT[:, :]).then_inc(gates_out, 16)
                    sp.wait_ge(gates_out, 16 * f + 16)
                    rows = gate_rows.rearrange("(b two) t -> two b t", two=2)
                    for n, k in enumerate(GATE_PARTS):
                        end = (GATE_PARTS + (BLOCKS,))[n + 1]
                        if g is not None and n == len(GATE_PARTS) - 1:
                            sp.wait_ge(yT_set, f + 1)
                        for half in range(2):
                            sp.dma_start(gate_bc[F * half:F * half + F, k:end, :],
                                         rows[half:half + 1, k:end].broadcast_to([F, end - k, TOK])
                                         ).then_inc(gates_in[n], 16)
                if g is not None:
                    sp.wait_ge(out_set, 4 * g + 4)
                    sp.dma_start(out_tiles[g], out_tok[:, :, :]).then_inc(stored, 16)

            turn(0, None, None, None)
            turn(1, 0, None, None)
            turn(2, 1, 0, None)
            with sp.Fori(3, TILES - 1) as i:
                turn(i, i - 1, i - 2, i - 3)
            turn(TILES - 1, TILES - 2, TILES - 3, TILES - 4, more_x=False)
            turn(None, TILES - 1, TILES - 2, TILES - 3, more_c=False)
            turn(None, None, TILES - 1, TILES - 2)
            turn(None, None, None, TILES - 1)
            sp.wait_ge(stored, 16 * TILES + 16)

        @block.tensor
        def _(pe):
            mm, tr = nc.tensor.matmul, nc.tensor.transpose

            pe.wait_ge(consts_in, 16)
            pe.wait_ge(raw_in, 16 * 7)
            for n in range(7):
                tr(A[n // 4][:, (n % 4) * P:(n % 4 + 1) * P], raw_w[:, n, :], ident).then_inc(w_turned, 1)

            def turned(dst, tok):
                for c in range(PAIRS):
                    last = tr(dst[:, c * P:(c + 1) * P], tok[:, c, :], ident)
                return last

            def token_values(src, w, dst):
                for c in range(PAIRS):
                    last = mm(dst[:, c * P:(c + 1) * P], src[:, c * P:(c + 1) * P], w, start=True, stop=True)
                return last

            def weighted_values(p, weights, dst):
                for b in range(2):
                    for e in range(2):
                        for q in range(QUADS):
                            last = mm(dst[32 * q:32 * q + 32, b * S:(b + 1) * S],
                                      v_pad[:, b, p * QUADS + q, 2 * e:2 * e + 2, :],
                                      weights(b, 2 * q + e), start=(e == 0), stop=(e == 1))
                return last

            def retained_values(p, dst):
                for q in range(2):
                    for head in range(4):
                        for half in range(2):
                            last = mm(dst[64 * half:64 * half + 64, q * S:(q + 1) * S],
                                      v2_pad[:, p, 2 * half + q, head * 64:head * 64 + 64],
                                      simT[half][:, (4 * q + head) * S:(4 * q + head + 1) * S],
                                      start=(head == 0), stop=(head == 3))
                return last

            def hidden_of(f, k):
                if k == 0:
                    pe.wait_ge(h_set[2], f + 1)
                    pe.wait_ge(x2T_split, 2 * f + 2)
                    pe.wait_ge(keys_split, 2)
                    pe.wait_ge(experts_in, 16 * 2)
                if k == 1:
                    pe.wait_ge(gatesT_set, f + 1)
                if k >= 2:
                    pe.wait_ge(hid_set, 16 * f + k - 1)
                hi, lo = keys_hi[:, k * P:(k + 1) * P], keys_lo[:, k * P:(k + 1) * P]
                mm(HB[k % 2][:, :], hi, x2T_hi[:, :], start=True, stop=False)
                mm(HB[k % 2][:, :], hi, x2T_lo[:, :], start=False, stop=False)
                mm(HB[k % 2][:, :], lo, x2T_hi[:, :], start=False, stop=True).then_inc(pe_hid, 1)

            def to_experts(f, k):
                if k >= 1:
                    hidden_of(f, k)
                    from_experts(f, k - 1)

            def from_experts(f, k):
                if k == 0:
                    pe.wait_ge(yT_set, f + 1)
                pe.wait_ge(hid_set, 16 * f + k + 1)
                mm(Y[:, :], vals_sb[:, k, :], hidden[k % 2][:, :],
                   start=(k == 0), stop=(k == BLOCKS - 1)).then_inc(pe_y, 1)

            def turn(a, t, f, g):
                def fill(part_, step):
                    tile = g if part_ == "joint" else f
                    if tile is not None:
                        for k in blocks_at(part_, step):
                            to_experts(tile, k)

                fill("joint", "begin")
                if t is not None:
                    pe.wait_ge(wide_set, t + 1)
                    for c in range(PAIRS):
                        last = tr(A[1][:, c * P:(c + 1) * P], inv_wide[:, c, :, :], ident)
                    last.then_inc(pe_inv, 1)
                if f is not None:
                    pe.wait_ge(sq_set, f + 1)
                    mm(R[1][:, :], head_mean, ret_sq[:, :], start=True, stop=True).then_inc(pe_var, 1)
                fill("joint", "inverse")
                if t is not None:
                    pe.wait_ge(attnT_set, t + 1)
                    pe.wait_ge(raw_set, 4 * t + 4)
                    for c in range(PAIRS):
                        last = mm(A[0][:, c * P:(c + 1) * P], attnT[:, c * P:(c + 1) * P], woT,
                                  start=True, stop=True)
                    last.then_inc(pe_o, 1)
                fill("joint", "project")
                if a is not None:
                    pe.wait_ge(x_in, 16 * a + 16)
                    after(pe, h_set[0], a)
                    turned(A[0], x_tok).then_inc(pe_xT, 1)
                if t is not None:
                    pe.wait_ge(c_in, 16 * t + 16)
                    after(pe, ret_set, 4 * t)
                    turned(R[0], c_tok).then_inc(pe_cT, 1)
                fill("joint", "variance")
                if a is not None:
                    pe.wait_ge(xT_set, a + 1)
                    if f is not None:
                        pe.wait_ge(gate_set, f + 1)
                    mm(M[:, :], wqT, xT[:, :], start=True, stop=True).then_inc(pe_q, 1)
                    mm(A[0][:, :], wkT, xT[:, :], start=True, stop=True).then_inc(pe_k, 1)
                if t is not None:
                    pe.wait_ge(cT_set, t + 1)
                    pe.wait_ge(w_rot, 4)
                    pe.wait_ge(w_mean, 3)
                    mm(R[0][:, :], wk2[:, :], cT[:, :], start=True, stop=True).then_inc(pe_k2, 1)
                if f is not None:
                    pe.wait_ge(gvar_set, f + 1)
                    pe.wait_ge(gated_set, f + 1)
                    for c in range(PAIRS):
                        last = mm(R[1][:, c * P:(c + 1) * P], gated[:, c * P:(c + 1) * P], wouT,
                                  start=True, stop=True)
                    last.then_inc(pe_out, 1)
                if a is not None:
                    pe.wait_ge(kT_set, a + 1)
                    token_values(xT, wvT, A[0]).then_inc(pe_v, 1)
                if t is not None:
                    pe.wait_ge(x1_set, 4 * t + 4)
                    turned(A[1], x1_tok).then_inc(pe_x1T, 1)
                if t is not None:
                    if f is not None:
                        pe.wait_ge(h_set[1], f + 1)
                    mm(R[1][:, :], wk2r[:, :], cT[:, :], start=True, stop=True).then_inc(pe_k2, 1)
                if t is not None:
                    pe.wait_ge(x1T_set, t + 1)
                    if a is not None:
                        pe.wait_ge(qT_set, a + 1)
                    mm(M[:, :], wq2[:, :], x1T[:, :], start=True, stop=True).then_inc(pe_q2, 1)
                fill("joint", "late")
                if f is not None:
                    pe.wait_ge(x2_set, 4 * f + 4)
                    turned(A[1], x2_tok).then_inc(pe_x2T, 1)
                if t is not None:
                    pe.wait_ge(k2_mul, 2 * t + 2)
                    mm(R[1][:, :], wq2r[:, :], x1T[:, :], start=True, stop=True).then_inc(pe_q2, 1)
                if t is not None:
                    pe.wait_ge(k2_mul, 2 * t + 1)
                    token_values(cT, wv2c[:, :], R[0]).then_inc(pe_v2, 1)
                if a is not None:
                    pe.wait_ge(v_set, 4 * a + 4)
                    pe.wait_ge(k_exp_set, 4 * a + 1)
                if f is not None:
                    pe.wait_ge(x2T_set, f + 1)
                    for c in range(PAIRS):
                        last = mm(A[1][:, c * E:(c + 1) * E], x2T[:, c * P:(c + 1) * P], selT[:, 0:E],
                                  start=True, stop=True)
                    last.then_inc(pe_sel, 1)
                fill("joint", "after")

                for p in range(PAIRS):
                    if a is not None:
                        if p == 0:
                            wait_apart(pe, w_copied, 2, qT_set, a + 1)
                            if f is not None:
                                pe.wait_ge(sel_exp, f + 1)
                        for half in HALVES:
                            if half == 0 and p > 0:
                                wait_apart(pe, w_copied, 2, raw_set, 4 * a + p)
                            rows = slice(64 * half, 64 * half + 64)
                            for b in range(2):
                                last = mm(A[half][b * S:(b + 1) * S, :], qT[rows, (2 * p + b) * S:(2 * p + b + 1) * S],
                                          k_exp[rows, p % 2, :, b * S:(b + 1) * S], start=True, stop=True)
                            last.then_inc(pe_scores, 1)
                    if t is not None and p == 0:
                        pe.wait_ge(q2_mul, 2 * t + 2)
                        mm(M[:, :], wgT, x1T[:, :], start=True, stop=True).then_inc(pe_gate, 1)
                        pe.wait_ge(q2_exp_set, 4 * t + 1)
                        pe.wait_ge(v2_set, 2 * t + 2)
                        pe.wait_ge(k2_set, t + 1)
                    if f is not None and p == 0:
                        pe.wait_ge(gates_set, f + 1)
                        if g is not None:
                            pe.wait_ge(hid_set, 16 * g + 16)
                        tr(HB[1][:, 0:P], gates[:, :, :], ident).then_inc(pe_gates, 1)
                    fill(f"pair{p}", "scores")
                    if t is not None:
                        for half in HALVES:
                            if half == 0 and p > 0:
                                wait_apart(pe, w_copied, 2, ret_set, 4 * t + p)
                            rows = slice(64 * half, 64 * half + 64)
                            for b in range(2):
                                last = mm(R[half][b * S:(b + 1) * S, :], k2T[rows, (2 * p + b) * S:(2 * p + b + 1) * S],
                                          q2_exp[rows, p % 2, :, b * S:(b + 1) * S], start=True, stop=True)
                            last.then_inc(pe_sim, 1)
                    if g is not None and p == 0:
                        from_experts(g, BLOCKS - 1)
                    fill(f"pair{p}", "sims")
                    if a is not None:
                        for n, half in enumerate(HALVES):
                            pe.wait_ge(exp_set, 8 * a + 2 * p + n + 1)
                            for c in range(4):
                                last = tr(A[half][:, c * P:(c + 1) * P], probs[half][:, c * P:(c + 1) * P], ident)
                            last.then_inc(pe_probsT, 1)
                    if g is not None and p == 0:
                        pe.wait_ge(yT_set, g + 2)
                        for c in range(PAIRS):
                            last = tr(HB[0][:, c * P:(c + 1) * P], yT[:, c * P:(c + 1) * P], ident)
                        last.then_inc(pe_ytok, 1)
                    if t is not None:
                        pe.wait_ge(decayed, 8 * t + 2 * p + 2)
                        retained_values(p, R[0]).then_inc(pe_ret, 1)
                    fill(f"pair{p}", "ret")
                    if t is not None and p + 1 < PAIRS:
                        pe.wait_ge(q2_exp_set, 4 * t + p + 2)
                    if a is not None:
                        pe.wait_ge(probsT_set, 8 * a + 2 * p + 2)
                        if p + 1 < PAIRS:
                            pe.wait_ge(k_exp_set, 4 * a + p + 2)
                        weighted_values(p, lambda b, hp: probsT[hp // 4][
                            :, (hp % 4) * P + b * S:(hp % 4) * P + (b + 1) * S], A[0]).then_inc(pe_attn, 1)
                    if f is not None and p == 0:
                        hidden_of(f, 0)
                    fill(f"pair{p}", "weighted")

            pe.wait_ge(w_copied, 2)
            over_tiles(pe, turn)

        @block.scalar
        def _(act):
            run = nc.scalar.activation
            act.preload_act_table_set("natural_log_exp_and_others")
            for n in range(2):
                w = (4, 3)[n]
                act.wait_ge(w_turned, (4, 7)[n])
                run(wT[:, 4 * n:4 * n + w, :], A[n][:, 0:w * P], ACT.Copy).then_inc(w_copied, 1)
            act.wait_ge(bias_in, 32)
            run(gb_neg[:, :], gb[:, :], ACT.Copy, scale=-1.0).then_inc(w_copied, 1)
            act.wait_ge(w_copied, 3)
            act.sem_inc(yT_set, 1)
            act.wait_ge(pads_set, 2)

            def values_out():
                for h2 in range(2):
                    d = slice(HD * h2, HD * h2 + HD)
                    for b in range(2):
                        own = A[0][S * b:S * b + S, :].rearrange("p (n e d) -> p n e d", e=2, d=16)
                        run(v_pad[64 * h2:64 * h2 + 64, b, :, 0:4:3, d], own[:, :, :, d], ACT.Copy).then_inc(v_set, 1)

            def root(n, i):
                act.wait_ge(mo_set[n], 4 * i + 4)
                run(var_ln[n][:, :], moments[n][:, :, 1:2].rearrange("p c o -> p (c o)"), ACT.Ln,
                    bias=eps).then_inc(ln_set[n], 1)
                act.wait_ge(ln_set[n], i + 1)
                run(rstd[n][:, :], var_ln[n][:, :], ACT.Exp, scale=-0.5).then_inc(rs_set[n], 1)

            def turn(a, t, f, g):
                if f is not None:
                    act.wait_ge(ret_set, 4 * f + 4)
                    run(ret_sq[:, :], ret_sep[:, :], ACT.Square).then_inc(sq_set, 1)
                if f is not None:
                    act.wait_ge(pe_var, f + 1)
                    run(grs[:, :], R[1][:, :], ACT.Ln, bias=eps).then_inc(gvar_set, 1)
                    act.wait_ge(gvar_set, f + 1)
                    run(grs[:, :], grs[:, :], ACT.Exp, scale=-0.5).then_inc(grs_set, 1)
                if t is not None:
                    root(0, t)
                if a is not None:
                    act.wait_ge(pe_xT, a + 1)
                    run(xT[:, :], A[0][:, :], ACT.Copy).then_inc(xT_set, 1)
                if t is not None:
                    act.wait_ge(pe_cT, t + 1)
                    run(cT[:, :], R[0][:, :], ACT.Copy).then_inc(cT_set, 1)
                if a is not None:
                    act.wait_ge(pe_k, a + 1)
                    run(kT[:, :], A[0][:, :], ACT.Copy).then_inc(kT_set, 1)
                    act.wait_ge(pe_q, a + 1)
                    run(qT[:, :], M[:, :], ACT.Copy).then_inc(qT_set, 1)
                if t is not None:
                    act.wait_ge(pe_x1T, t + 1)
                    run(x1T[:, :], A[1][:, :], ACT.Copy).then_inc(x1T_set, 1)
                if a is not None:
                    act.wait_ge(pe_v, a + 1)
                    values_out()
                if f is not None:
                    root(1, f)
                if f is not None:
                    act.wait_ge(pe_x2T, f + 1)
                    run(x2T[:, :], A[1][:, :], ACT.Copy).then_inc(x2T_set, 1)
                    act.wait_ge(pe_sel, f + 1)
                    run(sel_e[:, :, :], A[1][:, 0:PAIRS * E], ACT.Exp, scale=-1.0).then_inc(sel_exp, 1)
                if t is not None:
                    act.wait_ge(pe_v2, t + 1)
                    for b in range(2):
                        rows = slice(S * b, S * b + S)
                        own = v2_pad[rows, :, :, :].rearrange("p c n (h w) -> p (c n) h w", w=72)
                        run(own[:, :, :, 32 * b:32 * b + HD],
                            R[0][rows, :].rearrange("p (m h d) -> p m h d", h=4, d=HD), ACT.Copy).then_inc(v2_set, 1)
                if a is not None:
                    act.wait_ge(x_in, 16 * a + 16)
                    after(act, h_set[0], a)
                    run(xr_tok[:, :, :], x_tok[:, :, :], ACT.Copy).then_inc(xr_set, 1)
                if t is not None:
                    act.wait_ge(pe_gate, t + 1)
                    run(sw[:, :], M[:, :], ACT.Exp, scale=-1.0, bias=gb_neg[:, :]).then_inc(sw_exp, 1)
                if f is not None:
                    act.wait_ge(pe_gates, f + 1)
                    after(act, gates_out, 16 * f)
                    run(gatesT[:, :], HB[1][:, 0:P], ACT.Copy).then_inc(gatesT_set, 1)
                if f is not None:
                    act.wait_ge(x2T_set, f + 1)
                    if g is not None:
                        act.wait_ge(pe_hid, 16 * g + 16)
                    run(x2T_hi[:, :], x2T[:, :], ACT.Copy).then_inc(x2T_split, 1)
                for p in range(PAIRS):
                    if a is not None:
                        for n, half in enumerate(HALVES):
                            act.wait_ge(shifted, 8 * a + 2 * p + n + 1)
                            run(probs[half][:, :], probs[half][:, :], ACT.Exp, scale=SCALE).then_inc(exp_set, 1)
                    if g is not None and p == 0:
                        act.wait_ge(pe_y, 16 * g + 16)
                        run(yT[:, :], Y[:, :], ACT.Copy).then_inc(yT_set, 1)
                    if a is not None:
                        for n, half in enumerate(HALVES):
                            act.wait_ge(pe_probsT, 8 * a + 2 * p + n + 1)
                            run(probsT[half][:, :], A[half][:, :], ACT.Copy).then_inc(probsT_set, 1)
                    if t is not None and p == 0:
                        act.wait_ge(sw_exp, t + 1)
                        run(sw[:, :], sw[:, :], ACT.Ln, bias=one).then_inc(sw_log, 1)
                        act.wait_ge(sw_log, t + 1)
                        run(sw[:, :], sw[:, :], ACT.Exp, scale=-1.0).then_inc(sw_inv, 1)
                    if t is not None:
                        act.wait_ge(pe_ret, 4 * t + p + 1)
                        run(ret_sep[:, p * P:(p + 1) * P], R[0][:, 0:P], ACT.Copy).then_inc(ret_set, 1)
                    if a is not None:
                        act.wait_ge(pe_attn, 4 * a + p + 1)
                        run(rawT[:, p * P:(p + 1) * P], A[0][:, 0:P], ACT.Copy).then_inc(raw_set, 1)
                    if g is not None and p == 0:
                        root(2, g)
                if t is None and a is not None:
                    act.wait_ge(experts_in, 16 * 2)
                    run(keys_hi[:, :], gate_bc[:, 0:E * F // TOK, :], ACT.Copy).then_inc(keys_split, 1)
                if a is not None:
                    act.wait_ge(inv_set, a + 1)
                    wide = row_inv[:, :, :].rearrange("p c h -> p (c h)").rearrange("p (a o) -> p a o", o=1)
                    run(inv_wide[:, :, :, :].rearrange("p c h d -> p (c h) d"),
                        wide.broadcast_to([P, PAIRS * H, HD]), ACT.Copy).then_inc(wide_set, 1)

            over_tiles(act, turn)

        @block.vector
        def _(dve):
            v = nc.vector
            v.memset(raw_w[:, 6, :], 0.0).then_inc(raw_zero, 1)
            v.memset(sel_g[:, :, E:E + MAX8 - TOP], -1.0).then_inc(zeros_set, 1)
            v.memset(tops[:, :, :], -1.0).then_inc(zeros_set, 1)
            dve.wait_ge(zeros_set, 2)
            dve.wait_ge(w2_in, 16 * 3)
            for w, wr in ((wq2, wq2r), (wk2, wk2r)):
                even_odd = w[:, :].rearrange("p (n two) -> p n two", two=2)
                rotated = wr[:, :].rearrange("p (n two) -> p n two", two=2)
                v.tensor_scalar(rotated[:, :, 0:1], even_odd[:, :, 1:2], -1.0, None, ALU.mult).then_inc(w_rot, 1)
                v.tensor_copy(rotated[:, :, 1:2], even_odd[:, :, 0:1]).then_inc(w_rot, 1)
            heads = wv2[:, :].rearrange("p (h e) -> p h e", e=HD)
            v.tensor_reduce(head_sum[:, 0, :], heads, axis=AX.X, op=ALU.add).then_inc(w_mean, 1)
            dve.wait_ge(w_mean, 1)
            v.tensor_scalar(head_sum[:, 1, :], head_sum[:, 0, :], 1.0 / HD, None, ALU.mult).then_inc(w_mean, 1)
            dve.wait_ge(w_mean, 2)
            v.tensor_tensor(wv2c[:, :].rearrange("p (h e) -> p h e", e=HD), heads,
                            head_sum[:, 1, :].rearrange("p (h o) -> p h o", o=1).broadcast_to([P, H, HD]),
                            ALU.subtract).then_inc(w_mean, 1)
            dve.wait_ge(consts_in, 16)
            dve.wait_ge(bias_in, 32)
            dve.sem_inc(h_set[2], 1)

            def norm_stats(n, i):
                for c in range(PAIRS):
                    v.bn_stats(stats[n][:, c, :], h_tok[n][:, c, :]).then_inc(st_set[n], 1)
                dve.wait_ge(st_set[n], 4 * i + 4)
                v.memset(spare[:, :], 0.0)
                for c in range(PAIRS):
                    v.bn_aggr(moments[n][:, c, :], stats[n][:, c, :]).then_inc(mo_set[n], 1)

            def norm_apply(n, i, dst, done):
                dve.wait_ge(mo_set[n], 4 * i + 4)
                dve.wait_ge(rs_set[n], i + 1)
                for c in range(PAIRS):
                    v.tensor_scalar(dst[:, c, :], h_tok[n][:, c, :], moments[n][:, c, 0:1], rstd[n][:, c:c + 1],
                                    ALU.subtract, ALU.mult).then_inc(done, 1)

            def gate_block(f, k):
                if k in GATE_PARTS:
                    dve.wait_ge(gates_in[GATE_PARTS.index(k)], 32 * f + 32)
                dve.wait_ge(pe_hid, 16 * f + k + 1)
                if k >= 2:
                    dve.wait_ge(pe_y, 16 * f + k - 1)
                v.scalar_tensor_tensor(out=hidden[k % 2][:, :], in0=HB[k % 2][:, :], scalar=0.0,
                                       in1=gate_bc[:, k, :], op0=ALU.max, op1=ALU.mult).then_inc(hid_set, 1)

            def over_seqs(ap):
                return ap.rearrange("p (a t) -> p a t", a=1).broadcast_to([P, SEQS, S])

            def seqs(ap):
                return ap.rearrange("p (a t) -> p a t", t=S)

            def toks(bank):
                return bank[:, :].rearrange("p (c d) -> p c d", c=PAIRS)

            def turn(a, t, f, g):
                def fill(part_, step):
                    tile = g if part_ == "joint" else f
                    if tile is not None:
                        for k in blocks_at(part_, step):
                            gate_block(tile, k)

                fill("joint", "begin")
                if t is not None:
                    dve.wait_ge(raw_set, 4 * t + 4)
                    dve.wait_ge(pe_inv, t + 1)
                    v.tensor_tensor(attnT[:, :], A[1][:, :], rawT[:, :], ALU.mult).then_inc(attnT_set, 1)
                fill("joint", "inverse")
                if t is not None:
                    dve.wait_ge(pe_o, t + 1)
                    dve.wait_ge(xr_set, t + 1)
                    v.tensor_tensor(h_tok[0][:, :, :], toks(A[0]), xr_tok[:, :, :], ALU.add).then_inc(h_set[0], 1)
                    dve.wait_ge(h_set[0], t + 1)
                    norm_stats(0, t)
                fill("joint", "project")
                if f is not None:
                    dve.wait_ge(grs_set, f + 1)
                    dve.wait_ge(gate_set, f + 1)
                    for half in range(2):
                        for b in range(2):
                            for q in range(2):
                                rows, n = slice(64 * half + 32 * b, 64 * half + 32 * b + 32), 2 * half + q
                                v.tensor_tensor(
                                    gated[32 * n:32 * n + 32, :].rearrange("p (c b s) -> p c b s", b=2, s=S)[:, :, b, :],
                                    ret_sep[rows, :].rearrange("p (c q s) -> p c q s", q=2, s=S)[:, :, q, :],
                                    grs[rows, :].rearrange("p (c q s) -> p c q s", q=2, s=S)[:, :, q, :],
                                    ALU.mult).then_inc(retT_set, 1)
                    dve.wait_ge(retT_set, 8 * f + 8)
                    v.tensor_tensor(gated[:, :], gated[:, :], gateT[:, :], ALU.mult).then_inc(gated_set, 1)
                fill("joint", "variance")
                if t is not None:
                    if f is not None:
                        dve.wait_ge(x1b_set, f + 1)
                        dve.wait_ge(pe_gate, f + 1)
                    norm_apply(0, t, x1_tok, x1_set)
                if t is not None:
                    dve.wait_ge(pe_k2, 2 * t + 1)
                    after(dve, k2_set, t)
                    v.tensor_tensor(seqs(k2c[:, :]), seqs(R[0][:, :]), over_seqs(k_cos), ALU.mult).then_inc(k2_mul, 1)
                if f is not None:
                    dve.wait_ge(pe_out, f + 1)
                    dve.wait_ge(x1b_set, f + 1)
                    v.tensor_tensor(h_tok[1][:, :, :], toks(R[1]), x1b_tok[:, :, :], ALU.add).then_inc(h_set[1], 1)
                    dve.wait_ge(h_set[1], f + 1)
                    norm_stats(1, f)
                if f is not None:
                    if g is not None:
                        dve.wait_ge(x2c_set, g + 1)
                    norm_apply(1, f, x2_tok, x2_set)
                if t is not None:
                    dve.wait_ge(pe_k2, 2 * t + 2)
                    v.tensor_tensor(seqs(k2s[:, :]), seqs(R[1][:, :]), over_seqs(k_sin), ALU.mult).then_inc(k2_mul, 1)
                    dve.wait_ge(pe_q2, 2 * t + 1)
                    v.tensor_tensor(seqs(q2c[:, :]), seqs(M[:, :]), over_seqs(q_cos), ALU.mult).then_inc(q2_mul, 1)
                if g is not None:
                    for k in blocks_at("joint", "late"):
                        gate_block(g, k)
                if t is not None:
                    dve.wait_ge(pe_q2, 2 * t + 2)
                    v.tensor_tensor(seqs(q2s[:, :]), seqs(R[1][:, :]), over_seqs(q_sin), ALU.mult).then_inc(q2_mul, 1)
                if f is not None:
                    dve.wait_ge(sel_exp, f + 1)
                    v.tensor_scalar(sel_d[:, :, :], sel_e[:, :, :], 1.0, None, ALU.add).then_inc(sel_add, 1)
                    dve.wait_ge(sel_add, f + 1)
                    v.reciprocal(sel_g[:, :, 0:E], sel_d[:, :, :]).then_inc(sel_inv, 1)
                    wait_apart(dve, zeros_set, 2, sel_inv, f + 1)
                    for c in range(PAIRS):
                        v.max(tops[:, c, :], sel_g[:, c, 0:E]).then_inc(top_set, 1)
                    dve.wait_ge(top_set, 4 * f + 4)
                    v.memset(tops[:, :, TOP:MAX8], -1.0).then_inc(top_cut, 1)
                    wait_apart(dve, zeros_set, 2, top_cut, f + 1)
                    for c in range(PAIRS):
                        v.match_replace(out=sel_m[:, c, :], in_to_replace=tops[:, c, :],
                                        in_values=sel_g[:, c, :], imm_value=0.0).then_inc(matched, 1)
                    dve.wait_ge(matched, 4 * f + 4)
                    v.tensor_tensor(gates[:, :, :], sel_g[:, :, 0:E], sel_m[:, :, 0:E],
                                    ALU.subtract).then_inc(gates_set, 1)
                if g is not None:
                    for k in blocks_at("joint", "after"):
                        gate_block(g, k)

                for p in range(PAIRS):
                    if a is not None:
                        for first, half in enumerate(HALVES):
                            n = 8 * a + 2 * p + first
                            dve.wait_ge(pe_scores, n + 1)
                            after(dve, sum_set, n - 1)
                            v.tensor_tensor(seqs(probs[half][:, :]), seqs(A[half][:, :]), over_seqs(causal),
                                            ALU.add).then_inc(masked, 1)
                            dve.wait_ge(masked, n + 1)
                            v.tensor_reduce(row_max[:, half, :], seqs(probs[half][:, :]), axis=AX.X,
                                            op=ALU.max).then_inc(max_set, 1)
                    fill(f"pair{p}", "scores")
                    if t is not None:
                        for n, half in enumerate(HALVES):
                            dve.wait_ge(pe_sim, 8 * t + 2 * p + n + 1)
                            v.tensor_tensor(simT[half][:, :], R[half][:, :], decay[:, 8 * half * S:8 * (half + 1) * S],
                                            ALU.mult).then_inc(decayed, 1)
                    fill(f"pair{p}", "sims")
                    if a is not None:
                        for n, half in enumerate(HALVES):
                            dve.wait_ge(exp_set, 8 * a + 2 * p + n + 1)
                            v.tensor_reduce(row_sum[:, p, half, :], seqs(probs[half][:, :]), axis=AX.X,
                                            op=ALU.add).then_inc(sum_set, 1)
                    if g is not None and p == 0:
                        dve.wait_ge(pe_ytok, g + 1)
                        dve.wait_ge(x2c_set, g + 1)
                        v.tensor_tensor(h_tok[2][:, :, :], toks(HB[0]), x2c_tok[:, :, :], ALU.add).then_inc(h_set[2], 1)
                        dve.wait_ge(h_set[2], g + 2)
                        norm_stats(2, g)
                    fill(f"pair{p}", "ret")
                    if a is not None and p == PAIRS - 1:
                        dve.wait_ge(sum_set, 8 * a + 8)
                        v.reciprocal(row_inv[:, :, :],
                                     row_sum[:, :, :, :].rearrange("p c g j -> p c (g j)")).then_inc(inv_set, 1)
                    fill(f"pair{p}", "weighted")
                    if t is not None and p == 0:
                        dve.wait_ge(sw_inv, t + 1)
                        v.scalar_tensor_tensor(out=gateT[:, :], in0=M[:, :], scalar=gb[:, :], in1=sw[:, :],
                                               op0=ALU.add, op1=ALU.mult).then_inc(gate_set, 1)
                    if g is not None and p == 0:
                        dve.wait_ge(stored, 16 * g + 16)
                        norm_apply(2, g, out_tok, out_set)
                if t is None and a is not None:
                    dve.wait_ge(experts_in, 16 * 2)
                    dve.wait_ge(keys_split, 1)
                    v.tensor_tensor(keys_lo[:, :], gate_bc[:, 0:E * F // TOK, :].rearrange("p b t -> p (b t)"),
                                    keys_hi[:, :].bitcast(f32), ALU.subtract).then_inc(keys_split, 1)

            over_tiles(dve, turn)

        @block.gpsimd
        def _(pool):
            gp = nc.gpsimd
            gp.memset(v_pad[:, :, :, :, :], 0.0).then_inc(pads_set, 1)
            gp.memset(v2_pad[:, :, :, :], 0.0).then_inc(pads_set, 1)
            pool.wait_ge(consts_in, 16)
            pool.wait_ge(bias_in, 32)

            def expand(src, p, dst, done):
                heads = src[:, p * P:(p + 1) * P].rearrange("p (a t) -> p a t", a=1).broadcast_to([P, 8, P])
                pick = head_pick.rearrange("p (a t) -> p a t", t=1).broadcast_to([P, 8, P])
                gp.tensor_tensor(dst[:, p % 2, :, :], heads, pick, ALU.mult).then_inc(done, 1)

            def turn(a, t, f, g):
                if a is not None:
                    pool.wait_ge(kT_set, a + 1)
                    expand(kT, 0, k_exp, k_exp_set)
                    expand(kT, 1, k_exp, k_exp_set)
                if t is not None:
                    pool.wait_ge(k2_mul, 2 * t + 2)
                    gp.tensor_tensor(k2T[:, :], k2c[:, :], k2s[:, :], ALU.add).then_inc(k2_set, 1)
                    pool.wait_ge(q2_mul, 2 * t + 2)
                    gp.tensor_tensor(q2T[:, :], q2c[:, :], q2s[:, :], ALU.add).then_inc(q2_set, 1)
                    pool.wait_ge(q2_set, t + 1)
                    expand(q2T, 0, q2_exp, q2_exp_set)
                for p in range(PAIRS):
                    if a is not None:
                        for n, half in enumerate(HALVES):
                            pool.wait_ge(max_set, 8 * a + 2 * p + n + 1)
                            top = row_max[:, half, :].rearrange("p (a o) -> p a o", o=1).broadcast_to([P, 8, S])
                            s = probs[half][:, :].rearrange("p (a t) -> p a t", t=S)
                            gp.tensor_tensor(s, s, top, ALU.subtract).then_inc(shifted, 1)
                    if f is not None and p == 0:
                        pool.wait_ge(x2T_split, 2 * f + 1)
                        gp.tensor_tensor(x2T_lo[:, :], x2T[:, :], x2T_hi[:, :].bitcast(f32),
                                         ALU.subtract).then_inc(x2T_split, 1)
                    if t is not None and p == 0:
                        expand(q2T, 1, q2_exp, q2_exp_set)
                    if t is not None and p + 2 < PAIRS:
                        pool.wait_ge(pe_sim, 8 * t + 2 * p + 2)
                        expand(q2T, p + 2, q2_exp, q2_exp_set)
                    if a is not None and p + 2 < PAIRS:
                        expand(kT, p + 2, k_exp, k_exp_set)
                    if g is not None and p == 1:
                        pool.wait_ge(h_set[2], g + 2)
                    if t is not None and p == 1:
                        pool.wait_ge(x1_set, 4 * t + 4)
                        if f is not None:
                            pool.wait_ge(x2_set, 4 * f + 4)
                        gp.tensor_tensor(x1b_tok[:, :, :], x1_tok[:, :, :],
                                         ob[:, :].rearrange("p (a d) -> p a d", a=1).broadcast_to([P, PAIRS, D]),
                                         ALU.add).then_inc(x1b_set, 1)
                    if f is not None and p == 1:
                        if t is None:
                            pool.wait_ge(x2_set, 4 * f + 4)
                        gp.tensor_copy(x2c_tok[:, :, :], x2_tok[:, :, :]).then_inc(x2c_set, 1)

            over_tiles(pool, turn)


def constant_table():
    import numpy as np
    P, S, H, HD = 128, 64, 16, 8
    p = np.arange(P)
    same_head = (p[:, None] // HD == p[None, :] // HD) / HD
    causal = np.where(np.arange(S)[None, :] <= (p % S)[:, None], 0.0, -3.0e38)
    f4 = np.float32
    gammas = (1.0 - np.exp(np.linspace(np.log(1.0 / 32.0), np.log(1.0 / 512.0), H).astype(f4))).astype(f4)
    dist = np.arange(S)[None, None, :] - (p % S)[:, None, None]
    decay = np.where(dist >= 0, gammas[None, :, None].astype(np.float64) ** np.maximum(dist, 0), 0.0)
    base = ((np.arange(0, HD, 2) + 0.4 * HD) / (1.4 * HD)).astype(f4).astype(np.float64)
    power = np.arange(-(S // 2), S - S // 2) / 512.0
    scale = base[None, :] ** power[:, None]
    inv_freq = (1.0 / 10000.0 ** (np.arange(HD // 2, dtype=f4) / f4(HD // 2))).astype(f4)
    ang = (np.arange(S, dtype=f4)[:, None] * inv_freq[None, :]).astype(np.float64)
    rows = (p % HD) // 2
    turns = [t[:, rows].T for t in (np.cos(ang) * scale, np.sin(ang) * scale,
                                    np.cos(ang) / scale, np.sin(ang) / scale)]
    pick = ((p // HD) % 8)[:, None] == np.arange(8)[None, :]
    return np.ascontiguousarray(np.concatenate(
        [np.eye(P), same_head, causal, decay.reshape(P, -1), *turns, pick,
         np.full((P, 1), 1e-5), np.ones((P, 1))], axis=1).astype(f4))


_INS = ["x", "ctx_1024", "L0_attn_q_proj", "L0_attn_k_proj", "L0_attn_v_proj", "L0_attn_o_proj",
        "L0_xattn_W_Q", "L0_xattn_W_K", "L0_xattn_W_V", "L0_xattn_g_w", "L0_xattn_g_b",
        "L0_xattn_out_w", "L0_xattn_out_b", "L0_ffn_expert_sel", "L0_ffn_keys", "L0_ffn_values"]


def kernel(**inputs):
    import numpy as np
    import concourse.bacc as bacc
    from concourse import mybir
    from concourse.bass_utils import run_bass_kernel_spmd as run

    nc = bacc.Bacc("TRN2", target_bir_lowering=False, num_devices=1)
    arrays, args = {}, []
    named = [(name, np.ascontiguousarray(inputs[name])) for name in _INS] + [("consts", constant_table())]
    for name, a in named:
        arrays[f"in_{name}"] = a
        args.append(nc.dram_tensor(f"in_{name}", a.shape, mybir.dt.from_np(a.dtype), kind="ExternalInput").ap())
    args.append(nc.dram_tensor("out_0", inputs["x"].shape, mybir.dt.float32, kind="ExternalOutput").ap())
    decoder_layer(nc, *args)
    r = run(nc, [arrays], core_ids=[0])
    return r.results[0]["out_0"]
```
